# Optimizing a Trainium2 kernel written in Bass

```python
import numpy as np
import jax
import jax.numpy as jnp

def _softmax(x, axis=-1):
    return jax.nn.softmax(x, axis=axis)

def _gelu(x):
    return jax.nn.gelu(x, approximate=True)

def _silu(x):
    return jax.nn.silu(x)

def _sigmoid(x):
    return jax.nn.sigmoid(x)

def _layernorm(x, axis=-1, eps=1e-05):
    m = jnp.mean(x, axis=axis, keepdims=True)
    v = jnp.var(x, axis=axis, keepdims=True)
    return (x - m) / jnp.sqrt(v + eps)

def _scatter_add(tgt, idx, src, axis=0):
    return tgt.at[idx].add(src)

def _segment_sum(src, seg, n):
    return jax.ops.segment_sum(src, seg, n)
kernel_name = 'mk_flamingo_gated_d1_seqx_r8_b7e4f5'

def setup_inputs(seed: int=0):
    np.random.seed(seed)
    _w = jnp.asarray

    def _rec_inputs():
        import jax
        import jax.numpy as jnp
        _rk = jax.random.key(seed)
        x = 7.22e-05 + 1 * jax.random.normal(jax.random.fold_in(_rk, 1), (2, 256, 128), jnp.float32)
        _lenS = 256 - jax.random.randint(jax.random.fold_in(_rk, 7), (2,), 0, max(1, 256 // 4) + 1, jnp.int32)
        _lenS2 = 512 - jax.random.randint(jax.random.fold_in(_rk, 8), (2,), 0, max(1, 512 // 4) + 1, jnp.int32)
        _ctx_1024P = jax.random.normal(jax.random.fold_in(_rk, 11), (2, 16, 128), jnp.float32)
        _ctx_1024c = jax.random.dirichlet(jax.random.fold_in(_rk, 511), 0.3 * jnp.ones((16,), jnp.float32), (2, 512))
        _ctx_1024t = jnp.einsum('bsk,bkd->bsd', _ctx_1024c, _ctx_1024P)
        _ctx_1024t = _ctx_1024t * jax.lax.rsqrt(jnp.mean(jnp.square(_ctx_1024t)) + 1e-12) * 0.953939
        ctx_1024 = 4.13588e-05 + 0.999923 * (_ctx_1024t + 0.3 * jax.random.normal(jax.random.fold_in(_rk, 611), (2, 512, 128), jnp.float32))
        _g = jax.random.normal(jax.random.fold_in(_rk, 9001), (2, 1), jnp.float32)
        _g = jnp.sign(_g) * jnp.maximum(jnp.abs(_g), 1.0) + (_g == 0) * 1.0
        g_xattn = _g[0]
        g_ffn = _g[1]
        return (x, ctx_1024, g_xattn, g_ffn)
    x, ctx_1024, g_xattn, g_ffn = _rec_inputs()

    def _L0_xattn_setup():
        import jax, jax.numpy as jnp
        import numpy as np
        D_MODEL = 128
        NHEAD = 16
        D_K = D_MODEL // NHEAD

        def _split_heads(x):
            B, S, _ = x.shape
            return x.reshape(B, S, NHEAD, D_K).transpose(0, 2, 1, 3)
        key = jax.random.key(seed)
        ks = jax.random.split(key, 11)
        B, S = (4, 256)
        s = 1.0 / np.sqrt(D_MODEL)
        return {'query': jax.random.normal(ks[0], (B, S, D_MODEL), jnp.float32), 'key': jax.random.normal(ks[1], (B, S, D_MODEL), jnp.float32), 'value': jax.random.normal(ks[2], (B, S, D_MODEL), jnp.float32), 'Wq': jax.random.normal(ks[3], (D_MODEL, D_MODEL), jnp.float32) * s, 'bq': jnp.zeros((D_MODEL,), jnp.float32), 'Wk': jax.random.normal(ks[4], (D_MODEL, D_MODEL), jnp.float32) * s, 'bk': jnp.zeros((D_MODEL,), jnp.float32), 'Wv': jax.random.normal(ks[5], (D_MODEL, D_MODEL), jnp.float32) * s, 'bv': jnp.zeros((D_MODEL,), jnp.float32), 'Wo': jax.random.normal(ks[6], (D_MODEL, D_MODEL), jnp.float32) * s, 'bo': jnp.zeros((D_MODEL,), jnp.float32)}
    _L0_xattn_all = _L0_xattn_setup()
    _L0_xattn_in = {k: v for k, v in _L0_xattn_all.items() if k in ('Wq', 'bq', 'Wk', 'bk', 'Wv', 'bv', 'Wo', 'bo')}
    del _L0_xattn_all

    def _L0_ffn_setup():
        import jax, jax.numpy as jnp
        import numpy as np
        B, S, D, F, E, TOP_K = (4, 256, 128, 512, 8, 2)
        LN_EPS = 1e-05
        key = jax.random.key(seed)
        ks = jax.random.split(key, 4)
        sc = lambda fan_in: 1.0 / np.sqrt(fan_in)
        return {'x': jax.random.normal(ks[0], (B, S, D), jnp.float32), 'W1': jax.random.normal(ks[1], (E, D, F), jnp.float32) * sc(D), 'b1': jnp.zeros((E, F), jnp.float32), 'W2': jax.random.normal(ks[2], (E, F, D), jnp.float32) * sc(F), 'b2': jnp.zeros((E, D), jnp.float32), 'Wr': jax.random.normal(ks[3], (D, E), jnp.float32) * sc(D), 'br': jnp.zeros((E,), jnp.float32), 'gamma': jnp.ones((D,), jnp.float32), 'beta': jnp.zeros((D,), jnp.float32)}
    _L0_ffn_all = _L0_ffn_setup()
    _L0_ffn_in = {k: v for k, v in _L0_ffn_all.items() if k in ('W1', 'b1', 'W2', 'b2', 'Wr', 'br', 'gamma', 'beta')}
    del _L0_ffn_all
    return {'x': x, 'ctx_1024': ctx_1024, 'g_xattn': g_xattn, 'g_ffn': g_ffn, 'L0_xattn_Wq': _L0_xattn_in['Wq'], 'L0_xattn_bq': _L0_xattn_in['bq'], 'L0_xattn_Wk': _L0_xattn_in['Wk'], 'L0_xattn_bk': _L0_xattn_in['bk'], 'L0_xattn_Wv': _L0_xattn_in['Wv'], 'L0_xattn_bv': _L0_xattn_in['bv'], 'L0_xattn_Wo': _L0_xattn_in['Wo'], 'L0_xattn_bo': _L0_xattn_in['bo'], 'L0_ffn_W1': _L0_ffn_in['W1'], 'L0_ffn_b1': _L0_ffn_in['b1'], 'L0_ffn_W2': _L0_ffn_in['W2'], 'L0_ffn_b2': _L0_ffn_in['b2'], 'L0_ffn_Wr': _L0_ffn_in['Wr'], 'L0_ffn_br': _L0_ffn_in['br'], 'L0_ffn_gamma': _L0_ffn_in['gamma'], 'L0_ffn_beta': _L0_ffn_in['beta']}

def reference(x, ctx_1024, g_xattn, g_ffn, L0_xattn_Wq, L0_xattn_bq, L0_xattn_Wk, L0_xattn_bk, L0_xattn_Wv, L0_xattn_bv, L0_xattn_Wo, L0_xattn_bo, L0_ffn_W1, L0_ffn_b1, L0_ffn_W2, L0_ffn_b2, L0_ffn_Wr, L0_ffn_br, L0_ffn_gamma, L0_ffn_beta):
    import jax
    import jax.numpy as jnp

    def _L0_xattn_ref(query, key, value, Wq, bq, Wk, bk, Wv, bv, Wo, bo):
        import jax, jax.numpy as jnp
        import numpy as np
        D_MODEL = 128
        NHEAD = 16
        D_K = D_MODEL // NHEAD

        def _split_heads(x):
            B, S, _ = x.shape
            return x.reshape(B, S, NHEAD, D_K).transpose(0, 2, 1, 3)
        q = _split_heads(query @ Wq.T + bq)
        k = _split_heads(key @ Wk.T + bk)
        v = _split_heads(value @ Wv.T + bv)
        scale = 1.0 / np.sqrt(D_K).astype(np.float32)
        scores = jnp.einsum('bhqd,bhkd->bhqk', q, k) * scale
        attn = jax.nn.softmax(scores, axis=-1)
        out = jnp.einsum('bhqk,bhkd->bhqd', attn, v)
        B, H, S, dk = out.shape
        out = out.transpose(0, 2, 1, 3).reshape(B, S, H * dk)
        return out @ Wo.T + bo

    def _L0_ffn_ref(x, W1, b1, W2, b2, Wr, br, gamma, beta):
        import jax, jax.numpy as jnp
        import numpy as np
        B, S, D, F, E, TOP_K = (4, 256, 128, 512, 8, 2)
        LN_EPS = 1e-05
        b, s, d = x.shape
        e = Wr.shape[1]
        rw = jax.nn.softmax(x.mean(axis=1) @ Wr + br, axis=-1)
        x_flat = x.reshape(-1, d)
        rw_tok = jnp.repeat(rw, s, axis=0)
        tk_w, tk_i = jax.lax.top_k(rw_tok, TOP_K)
        tk_w = jax.nn.softmax(tk_w, axis=-1)
        h = jax.nn.gelu(jnp.einsum('nd,edf->enf', x_flat, W1) + b1[:, None, :], approximate=False)
        expert_out = jnp.einsum('enf,efd->end', h, W2) + b2[:, None, :]
        onehot = jax.nn.one_hot(tk_i, e, dtype=x.dtype)
        cw = jnp.einsum('nk,nke->ne', tk_w, onehot)
        out = jnp.einsum('ne,end->nd', cw, expert_out).reshape(b, s, d)
        y = out + x
        mu = y.mean(axis=-1, keepdims=True)
        var = y.var(axis=-1, keepdims=True)
        return (y - mu) / jnp.sqrt(var + LN_EPS) * gamma + beta
    x = x + jnp.tanh(g_xattn[0]) * _L0_xattn_ref(_layernorm(x, axis=-1), ctx_1024, ctx_1024, L0_xattn_Wq, L0_xattn_bq, L0_xattn_Wk, L0_xattn_bk, L0_xattn_Wv, L0_xattn_bv, L0_xattn_Wo, L0_xattn_bo)
    x = x + jnp.tanh(g_ffn[0]) * _L0_ffn_ref(_layernorm(x, axis=-1), L0_ffn_W1, L0_ffn_b1, L0_ffn_W2, L0_ffn_b2, L0_ffn_Wr, L0_ffn_br, L0_ffn_gamma, L0_ffn_beta)
    return x

_drawn_inputs = setup_inputs


def setup_inputs(seed=0):
    import zlib

    import numpy as np

    out = dict(_drawn_inputs(seed))
    spreads = {'L0_xattn_bq': (0.0, 0.437),
     'L0_xattn_bk': (0.0, 0.8),
     'L0_xattn_bv': (0.0, 0.1),
     'L0_xattn_bo': (0.0, 0.1),
     'L0_ffn_b1': (0.0, 0.1),
     'L0_ffn_b2': (0.0, 0.1),
     'L0_ffn_br': (0.0, 0.1),
     'L0_ffn_gamma': (1.0, 0.2),
     'L0_ffn_beta': (0.0, 0.1)}
    factors = {}
    for name, (base, spread) in spreads.items():
        noise = np.random.default_rng([zlib.crc32(name.encode()), seed]).standard_normal(out[name].shape)
        drawn = base * np.exp(spread * noise) if base else spread * noise
        out[name] = jnp.asarray(drawn.astype(out[name].dtype))
    for name, factor in factors.items():
        out[name] = (out[name] * factor).astype(out[name].dtype)
    return out
```

```python
import concourse.bass as bass
from concourse import mybir
from contextlib import ExitStack
import math

B, S, C, D = 2, 256, 512, 128
H, DK = 16, 8
E, F = 8, 512
P = 128
QT, KT = S // P, C // P
FT = F // P
UNITS = B * H // 2
UPB = UNITS // B
QUADS = UNITS // 2
HB = 64
MAXROW = 48
CH = 4
RING = 3
SCALE = 1.0 / math.sqrt(DK)
EPS = 1e-5
ROWS = 6 * D + E + 2
COLS = E * FT + E + E

SMALL_IN = {4: ("O", 0), 6: ("O", 1), 8: ("O", 2), 10: ("O", 3), 11: ("attnT", 0), 12: ("O", 4),
            13: ("proj", 0), 14: ("O", 5), 15: ("h2T", 0)}
T1_ORDER = [("hT", 0)]
for _i in range(UNITS):
    T1_ORDER += [("max", _i)] + ([SMALL_IN[_i]] if _i in SMALL_IN else [])
T1_ORDER += [("router", 0), ("O", 6), ("O", 7), ("attnT", 1), ("proj", 1), ("h2T", 1), ("router", 1)]
T0_ORDER = [("hT", 1)] + [("stack", i) for i in range(UNITS)] + [("yT", 0), ("yT", 1)]
READERS = {"stack": 3, "yT": 2}


def uses_up_to(order, name):
    return order.index(name) + 1


def reads_before(order, name):
    return sum(READERS.get(n, 1) for n, _ in order[:order.index(name)])


def reads_up_to(order, name):
    return reads_before(order, name) + READERS.get(name[0], 1)


def build(nc, x, ctxT, wqkvo, w1, w2, cols, rows, out):
    f32, bf16, u32 = mybir.dt.float32, mybir.dt.bfloat16, mybir.dt.uint32
    ALU, ACT, AX = mybir.AluOpType, mybir.ActivationFunctionType, mybir.AxisListType
    ctx = ExitStack()
    with ctx:
        def sb(name, shape, dt=f32):
            return ctx.enter_context(nc.sbuf_tensor(name, shape, dt))

        def ps(name, shape, dt=f32):
            return ctx.enter_context(nc.psum_tensor(name, shape, dt))

        def sem(name):
            return ctx.enter_context(nc.semaphore(name))

        xs = sb("xs", [P, B * QT, D])
        cT = sb("cT", [P, B * KT * P])
        w = sb("w", [P, 4 * D])
        w1s = sb("w1s", [P, E * F])
        w2s = sb("w2s", [P, E * F])
        col = sb("col", [P, COLS])
        row = sb("row", [P, ROWS])
        bk, bv, bq, bo, gamma, beta = (row[:, n * D:(n + 1) * D] for n in (1, 2, 0, 3, 4, 5))
        br = row[:, 6 * D:6 * D + E]
        gates = row[:, 6 * D + E:ROWS]
        ident = sb("ident", [P, P])
        identb = sb("identb", [P, P], bf16)
        tg = sb("tg", [P, 2])
        xg = sb("xg", [P, B * QT, D])
        gam2 = sb("gam2", [P, D])
        bet2 = sb("bet2", [P, D])
        half = sb("half", [P, QT])
        euler = sb("euler", [P, E])
        LN = 3 * B
        stats = sb("stats", [P, LN, QT, 6])
        mv = sb("mv", [P, LN, QT, 2])
        veps = sb("veps", [P, LN, QT])
        rstd = sb("rstd", [P, LN, QT])
        h = sb("h", [P, B * QT, D])
        hT = sb("hT", [P, B * S])
        qf = sb("qf", [P, B * QT, D])
        qr = sb("qr", [P, B * QT, D])
        kf = sb("kf", [P, B * KT, D])
        kr = sb("kr", [P, B * KT, D])
        qst = sb("qst", [P, B * QT, H // 2, P], bf16)
        kst = sb("kst", [P, B * KT, H // 2, P], bf16)
        kT = sb("kT", [P, UNITS, C], bf16)
        qA = sb("qA", [P, RING, 2, S], bf16)
        qB = sb("qB", [P, RING, S], bf16)
        vx = sb("vx", [P, B * KT, H, 32])
        nmax = sb("nmax", [P, UNITS, CH])
        pr = sb("pr", [P, 2, 4, KT, S])
        oT = sb("oT", [P, 2, S])
        rs = sb("rs", [P, QUADS, QT, 4])
        attn = sb("attn", [P, B * QT, D])
        attnT = sb("attnT", [P, B, S])
        tbo = sb("tbo", [P, D])
        x2 = sb("x2", [P, B * QT, D])
        xo = sb("xo", [P, B * QT, D])
        h2 = sb("h2", [P, B * QT, D])
        h2T = sb("h2T", [P, B, S])
        hsum = sb("hsum", [P, B])
        rt = sb("rt", [P, B, 8, E])
        top = sb("top", [P, B, E])
        idx = sb("idx", [P, B, E], u32)
        sc = sb("sc", [P, B, 16])
        w1e = sb("w1e", [P, B, 2, F])
        w2e = sb("w2e", [P, B, 2, F])
        b1e = sb("b1e", [P, B, 2, FT])
        b2e = sb("b2e", [P, B, 2])
        hid = pr[:, 0, :, :, :].rearrange("p h k s -> p (h k) s").rearrange("p (b n) s -> p b n s", b=B)
        yT = sb("yT", [P, B, S])
        yn = sb("yn", [P, B * QT, D])
        yg = sb("yg", [P, B * QT, D])
        yo = sb("yo", [P, B * QT, D])

        bankA = [ps(f"bankA{n}", [P, 512]) for n in range(3)]
        bankB = [ps(f"bankB{n}", [P, 512]) for n in range(2)]
        bankV = ps("bankV", [P, 512])
        T0 = ps("T0", [P, 512])
        T1 = ps("T1", [P, 512])
        T0b = T0[:, :].bitcast(bf16)
        T1b = T1[:, :].bitcast(bf16)

        ld_x, ld_w, ld_row, ld_c0, ld_c1 = sem("ld_x"), sem("ld_w"), sem("ld_row"), sem("ld_c0"), sem("ld_c1")
        ld_col, ld_w1, ld_w2 = sem("ld_col"), sem("ld_w1"), sem("ld_w2")
        stored = sem("stored")
        ident_ready = sem("ident_ready")
        consts_ready = sem("consts_ready")
        pads_ready = sem("pads_ready")
        tanh_ready = sem("tanh_ready")
        folded = sem("folded")
        veps_ready, rstd_ready = sem("veps_ready"), sem("rstd_ready")
        h_ready = sem("h_ready")
        qp_done, kvp_done = sem("qp_done"), sem("kvp_done")
        qf_ready, kf_ready, vx_ready = sem("qf_ready"), sem("kf_ready"), sem("vx_ready")
        kpart = [sem(f"kpart{b}") for b in range(B)]
        qpart = [sem(f"qpart{b}") for b in range(B)]
        t0_filled, t0_read = sem("t0_filled"), sem("t0_read")
        t1_filled, t1_read = sem("t1_filled"), sem("t1_read")
        a_filled, a_read = sem("a_filled"), sem("a_read")
        m_high, m_ready = sem("m_high"), sem("m_ready")
        qmask_ready = sem("qmask_ready")
        qpads_ready = sem("qpads_ready")
        b_filled, p_ready = sem("b_filled"), sem("p_ready")
        pv_done, oT_ready = sem("pv_done"), sem("oT_ready")
        rs_ready = sem("rs_ready")
        h2_ready = sem("h2_ready")
        xo_ready = sem("xo_ready")
        z_ready, ez_ready = sem("z_ready"), sem("ez_ready")
        chosen = sem("chosen")
        w1e_ready, w2e_ready = sem("w1e_ready"), sem("w2e_ready")
        up_done, hid_ready, down_done = sem("up_done"), sem("hid_ready"), sem("down_done")
        yT_ready = sem("yT_ready")
        y_ready = sem("y_ready")
        chain = sem("chain")
        pchain = sem("pchain")

        upBank = [bankA[0], bankA[1], bankA[2], bankB[1]]
        downBank = [bankB[0], bankV]

        kst_blocks = kst[:, :, :, :].rearrange("p t g (j c) -> p (t g j) c", c=HB)
        qst_blocks = qst[:, :, :, :].rearrange("p t g (j c) -> p (t g j) c", c=HB)

        def heads(t, b, tiles):
            return t[:, b * tiles:(b + 1) * tiles, :].rearrange("p t (h d) -> p (t h) d", d=DK)

        def slots(blocks, b, tiles, first, step, count):
            part = blocks[:, b * tiles * H:(b + 1) * tiles * H, 0:MAXROW].rearrange("p n (s d) -> p n s d", d=DK)
            return part[:, :, first:first + step * (count - 1) + 1:step, :]

        def over(a, count):
            return a.unsqueeze(2).broadcast_to([P, a.shape[1], count, DK])

        QPARTS = [(0, 1, 3), (3, 2, 2), (4, 1, 1)]
        KPARTS = [(2, 1, 3), (1, 4, 2), (0, 1, 1)]

        def cut(step, copy, sub, blocks, full, rest, b, tiles, parts):
            high = slots(blocks, b, tiles, *parts[0])
            mid = slots(blocks, b, tiles, *parts[1])
            low = slots(blocks, b, tiles, *parts[2])
            v, r = heads(full, b, tiles), heads(rest, b, tiles)
            if step == 0:
                return copy(high, over(v, 3))
            if step == 1:
                return sub(r, v, high[:, :, 0, :])
            if step == 2:
                return copy(mid, over(r, 2))
            return sub(low[:, :, 0, :], r, mid[:, :, 0, :])

        block = ctx.enter_context(nc.Block())

        @block.sync
        def _(sp):
            sp.dma_start(xs[:, :, :], x.rearrange("p (t d) -> p t d", d=D)).then_inc(ld_x, 16)
            sp.dma_start(cT[:, 0:C], ctxT[:, 0:C]).then_inc(ld_c0, 16)
            sp.dma_start(cT[:, C:2 * C], ctxT[:, C:2 * C]).then_inc(ld_c1, 16)
            sp.dma_start(col[:, :], cols).then_inc(ld_col, 16)
            sp.dma_start(w1s[:, :], w1).then_inc(ld_w1, 16)
            sp.dma_start(w2s[:, :], w2).then_inc(ld_w2, 16)
            for b in range(B):
                for t in range(QT):
                    n = b * QT + t
                    sp.wait_ge(y_ready, n + 1)
                    sp.dma_start(out[n * P:(n + 1) * P, :], yo[:, n, :]).then_inc(stored, 16)
            sp.wait_ge(stored, 16 * B * QT)

        @block.gpsimd
        def _(pool):
            steps = [0]

            def link(ins):
                steps[0] += 1
                ins.then_inc(pchain, 1)
                pool.wait_ge(pchain, steps[0])

            pool.memset(half[:, :], -0.5).then_inc(consts_ready, 1)
            link(pool.memset(ident[:, :], 0.0))
            link(pool.affine_select(out=ident[:, :], in_=ident[:, :], compare_op=ALU.not_equal, fill=1.0,
                                    base=0, pattern=[[-1, P]], channel_multiplier=1))
            pool.tensor_copy(identb[:, :], ident[:, :]).then_inc(ident_ready, 1)
            pool.memset(kst_blocks[:, :, MAXROW:MAXROW + 2], 1.0).then_inc(pads_ready, 1)
            pool.memset(kst_blocks[:, :, MAXROW + 2:HB], 0.0).then_inc(pads_ready, 1)
            pool.memset(euler[:, :], math.e).then_inc(consts_ready, 1)

            def power(base, exponent, result, done):
                pool.tensor_tensor(result, base, exponent, ALU.pow).then_inc(done, 1)

            pool.wait_ge(consts_ready, 2)
            for b in range(B):
                pool.wait_ge(veps_ready, b + 1)
                power(veps[:, b, :], half[:, :], rstd[:, b, :], rstd_ready)
            pool.memset(vx[:, :, :, DK:DK + 1], 1.0).then_inc(pads_ready, 1)
            pool.memset(vx[:, :, :, DK + 1:32], 0.0).then_inc(pads_ready, 1)
            pool.wait_ge(ld_row, 16)
            pool.wait_ge(tanh_ready, 1)
            pool.wait_ge(ld_x, 16)
            pool.tensor_scalar(gam2[:, :], gamma, tg[:, 1:2], None, ALU.mult).then_inc(folded, 1)
            pool.tensor_scalar(bet2[:, :], beta, tg[:, 1:2], None, ALU.mult).then_inc(folded, 1)
            link(pool.tensor_scalar(tbo[:, :], bo, tg[:, 0:1], None, ALU.mult))
            pool.tensor_tensor(xg[:, :, :], xs[:, :, :], tbo[:, :].unsqueeze(1).broadcast_to([P, B * QT, D]),
                               ALU.add).then_inc(folded, 1)
            for full, rest, blocks, tiles, parts, ready, part in (
                    (qf, qr, qst_blocks, QT, QPARTS, qf_ready, qpart[1]),
                    (kf, kr, kst_blocks, KT, KPARTS, kf_ready, kpart[1])):
                pool.wait_ge(ready, 2 if tiles == QT else 4)
                for s in range(4):
                    if s:
                        pool.wait_ge(part, s)
                    cut(s, pool.tensor_copy,
                        lambda o, a, c: pool.tensor_tensor(o, a, c, ALU.subtract),
                        blocks, full, rest, 1, tiles, parts).then_inc(part, 1)
            for b in range(B):
                n = B + b
                pool.wait_ge(veps_ready, n + 1)
                power(veps[:, n, :], half[:, :], rstd[:, n, :], rstd_ready)
                pool.wait_ge(z_ready, 2 * b + 1)
                power(euler[:, :], rt[:, b, 1, :], rt[:, b, 2, :], ez_ready)
                pool.wait_ge(t1_read, reads_up_to(T1_ORDER, ("proj", b)))
                pool.wait_ge(folded, 3)
                pool.tensor_tensor(xo[:, b * QT:(b + 1) * QT, :], x2[:, b * QT:(b + 1) * QT, :],
                                   bet2[:, :].unsqueeze(1).broadcast_to([P, QT, D]), ALU.add).then_inc(xo_ready, 1)
                pool.wait_ge(z_ready, 2 * b + 2)
                power(euler[:, 0:1], sc[:, b, 2:3], sc[:, b, 3:4], ez_ready)
            for b in range(B):
                n = 2 * B + b
                pool.wait_ge(veps_ready, n + 1)
                power(veps[:, n, :], half[:, :], rstd[:, n, :], rstd_ready)

        @block.scalar
        def _(act):
            def act_copy(o, a):
                return nc.scalar.activation(o, a, ACT.Copy)

            act.dma_start(w[:, :], wqkvo).then_inc(ld_w, 16)
            act.dma_start(row[:, :], rows.partition_broadcast(P)).then_inc(ld_row, 16)
            act.wait_ge(ld_row, 16)
            nc.scalar.activation(tg[:, :], gates, ACT.Tanh).then_inc(tanh_ready, 1)
            for b in range(B):
                bank, filled, read, use = (T1, t1_filled, t1_read, 1) if b == 0 else (T0, t0_filled, t0_read, 1)
                act.wait_ge(filled, use)
                act_copy(hT[:, b * S:(b + 1) * S], bank[:, 0:S]).then_inc(read, 1)
            for s in (0, 2):
                for full, rest, blocks, tiles, parts, ready, part, count in (
                        (qf, qr, qst_blocks, QT, QPARTS, qf_ready, qpart[0], 1),
                        (kf, kr, kst_blocks, KT, KPARTS, kf_ready, kpart[0], 2)):
                    act.wait_ge(ready, count)
                    if s:
                        act.wait_ge(part, s)
                    cut(s, act_copy, None, blocks, full, rest, 0, tiles, parts).then_inc(part, 1)

            def stack_copy(i):
                act.wait_ge(t0_filled, uses_up_to(T0_ORDER, ("stack", i)))
                act_copy(kT[:, i, :], T0b[:, 0:C]).then_inc(t0_read, 1)
                if i >= RING:
                    act.wait_ge(a_filled, CH * (i - RING + 1))
                if i == 0:
                    act.wait_ge(qmask_ready, 1)
                for j in range(2):
                    act_copy(qA[j * HB:(j + 1) * HB, i % RING, j, :],
                             T0b[j * HB:(j + 1) * HB, C:C + S]).then_inc(t0_read, 1)

            def exps(i, k):
                q, j, half_ = i // 2, k // 2, k % 2
                act.wait_ge(b_filled, CH * i + k + 1)
                if q >= 2:
                    act.wait_ge(pv_done, q - 1)
                nc.scalar.activation(
                    pr[:, q % 2, (i % 2) * 2 + j, 2 * half_:2 * half_ + 2, :],
                    bankB[k % 2][:, :].rearrange("p (t s) -> p t s", t=2),
                    ACT.Exp, scale=SCALE).then_inc(p_ready, 1)

            def o_copy(q):
                act.wait_ge(pv_done, q + 1)
                if q >= 2:
                    act.wait_ge(t1_filled, uses_up_to(T1_ORDER, ("O", q - 2)))
                act_copy(oT[:, q % 2, :], bankV[:, 0:S]).then_inc(oT_ready, 1)

            def attnT_copy(b):
                act.wait_ge(t1_filled, uses_up_to(T1_ORDER, ("attnT", b)))
                act_copy(attnT[:, b, :], T1[:, 0:S]).then_inc(t1_read, 1)

            def h2T_copy(b):
                act.wait_ge(t1_filled, uses_up_to(T1_ORDER, ("h2T", b)))
                nc.scalar.activation(h2T[:, b, :], T1[:, 0:S], ACT.Copy,
                                     accum_out=hsum[:, b:b + 1]).then_inc(t1_read, 1)

            def pick_down(b):
                act.wait_ge(chosen, b + 1)
                act.wait_ge(ld_w2, 16)
                for s in range(2):
                    e = nc.scalar.value_load(idx[0:1, b, s:s + 1], min_val=0, max_val=E - 1)
                    nc.scalar.activation(w2e[:, b, s, :], w2s[:, bass.ds(e * F, F)], ACT.Copy,
                                         scale=sc[:, b, 5 + s:6 + s]).then_inc(w2e_ready, 1)

            def gelu(b, n):
                act.wait_ge(up_done, 2 * FT * b + n + 1)
                nc.scalar.activation(hid[:, b, n, :], upBank[n % 4][:, 0:S], ACT.Gelu,
                                     bias=b1e[:, b, n // FT, n % FT:n % FT + 1]).then_inc(hid_ready, 1)

            for i in range(RING):
                stack_copy(i)
            for i in range(UNITS):
                exps(i, 0)
                exps(i, 1)
                exps(i, 2)
                if SMALL_IN.get(i) == ("attnT", 0):
                    attnT_copy(0)
                if SMALL_IN.get(i) == ("h2T", 0):
                    h2T_copy(0)
                exps(i, 3)
                if i >= 3 and i % 2 == 1:
                    o_copy((i - 3) // 2)
                if i + RING < UNITS:
                    stack_copy(i + RING)
            o_copy(7)
            pick_down(0)
            for n in range(2 * FT):
                if n == 0:
                    attnT_copy(1)
                gelu(0, n)
                if n == 3:
                    h2T_copy(1)
            pick_down(1)
            for n in range(2 * FT):
                gelu(1, n)

        @block.vector
        def _(dve):
            steps = [0]

            def link(ins):
                steps[0] += 1
                ins.then_inc(chain, 1)
                dve.wait_ge(chain, steps[0])

            def norm_stats(n, source, b):
                for t in range(QT):
                    last = nc.vector.bn_stats(stats[:, n, t, :], source(t))
                    if t == QT - 1:
                        link(last)
                    else:
                        steps[0] += 1
                        last.then_inc(chain, 1)
                for t in range(QT):
                    last = nc.vector.bn_aggr(mv[:, n, t, :], stats[:, n, t, :])
                    if t == QT - 1:
                        link(last)
                    else:
                        steps[0] += 1
                        last.then_inc(chain, 1)
                nc.vector.tensor_scalar(veps[:, n, :], mv[:, n, :, 1], EPS, None, ALU.add).then_inc(veps_ready, 1)

            def normalise(n, target, source, b, done):
                dve.wait_ge(rstd_ready, n + 1)
                for t in range(QT):
                    nc.vector.tensor_scalar(target[:, b * QT + t, :], source(t), mv[:, n, t, 0:1],
                                            rstd[:, n, t:t + 1], ALU.subtract, ALU.mult).then_inc(done, 1)

            nc.vector.memset(qA[:, :, :, :].rearrange("p r j s -> p (r j s)").bitcast(u32), 0).then_inc(qmask_ready, 1)
            nc.vector.memset(qst_blocks[:, :, MAXROW:HB], 0.0).then_inc(qpads_ready, 1)
            dve.wait_ge(ld_x, 16)
            for b in range(B):
                norm_stats(b, lambda t: xs[:, b * QT + t, :], b)
            for b in range(B):
                normalise(b, h, lambda t: xs[:, b * QT + t, :], b, h_ready)

            def q_bias(b):
                dve.wait_ge(qp_done, b + 1)
                bank = bankA[2] if b == 0 else bankV
                nc.vector.tensor_tensor(qf[:, b * QT:(b + 1) * QT, :],
                                        bank[:, 0:S].rearrange("p (t d) -> p t d", d=D),
                                        bq.unsqueeze(1).broadcast_to([P, QT, D]), ALU.add).then_inc(qf_ready, 1)

            def kv_view(n):
                bank = bankA[n] if n < 2 else bankB[n - 2]
                return bank[:, :].rearrange("p (t d) -> p t d", d=2 * D)

            def k_bias(n):
                dve.wait_ge(kvp_done, n + 1)
                nc.vector.tensor_tensor(kf[:, 2 * n:2 * n + 2, :], kv_view(n)[:, :, 0:D],
                                        bk.unsqueeze(1).broadcast_to([P, 2, D]), ALU.add).then_inc(kf_ready, 1)

            def v_bias(n):
                if n == 0:
                    dve.wait_ge(pads_ready, 4)
                for t in range(2):
                    nc.vector.tensor_tensor(vx[:, 2 * n + t, :, 0:DK],
                                            kv_view(n)[:, t, D:2 * D].rearrange("p (h d) -> p h d", d=DK),
                                            bv.rearrange("p (h d) -> p h d", d=DK), ALU.add).then_inc(vx_ready, 1)

            dve.wait_ge(ld_row, 16)
            q_bias(0)
            k_bias(0)
            k_bias(1)
            sub = lambda o, a, c: nc.vector.tensor_tensor(o, a, c, ALU.subtract)
            for s in (1, 3):
                for full, rest, blocks, tiles, parts, part, ready, n in (
                        (qf, qr, qst_blocks, QT, QPARTS, qpart[0], qf_ready, 1),
                        (kf, kr, kst_blocks, KT, KPARTS, kpart[0], kf_ready, 2)):
                    dve.wait_ge(part, s)
                    cut(s, None, sub, blocks, full, rest, 0, tiles, parts).then_inc(part, 1)
                if s == 1:
                    v_bias(0)
                    v_bias(1)
            q_bias(1)
            k_bias(2)
            k_bias(3)
            v_bias(2)
            v_bias(3)

            def row_max(i, k):
                c = CH * i + k
                dve.wait_ge(a_filled, c + 1)
                nc.vector.reduce_max(nmax[:, i, k:k + 1], bankA[c % 3][:, :], axis=AX.X,
                                     negate=True).then_inc(a_read, 1)

            def put_max(i):
                b, g = divmod(i, UPB)
                cols_ = qst[:, b * QT:(b + 1) * QT, g, :].rearrange("p t (j c) -> p j t c", c=HB)
                m = nmax[:, i, :].rearrange("p (j t) -> p j t", j=2)
                dve.wait_ge(a_read, CH * (i + 1))
                nc.vector.tensor_copy(cols_[:, :, :, MAXROW], m).then_inc(m_high, 1)
                dve.wait_ge(m_high, i + 1)
                nc.vector.tensor_tensor(cols_[:, :, :, MAXROW + 1], m, cols_[:, :, :, MAXROW],
                                        ALU.subtract).then_inc(m_ready, 1)

            def qB_copy(i):
                dve.wait_ge(t1_filled, uses_up_to(T1_ORDER, ("max", i)))
                if i >= RING:
                    dve.wait_ge(b_filled, CH * (i - RING + 1))
                nc.vector.tensor_copy(qB[:, i % RING, :], T1b[:, 0:S]).then_inc(t1_read, 1)

            def o_norm(q):
                b, quad = divmod(q, QUADS // B)
                dve.wait_ge(t1_filled, uses_up_to(T1_ORDER, ("O", q)))
                o = T1[:, 0:S].rearrange("p (t h c) -> p t h c", t=QT, h=4)
                nc.vector.reciprocal(rs[:, q, :, :], o[:, :, :, DK]).then_inc(rs_ready, 1)
                dve.wait_ge(rs_ready, q + 1)
                target = attn[:, b * QT:(b + 1) * QT, 32 * quad:32 * quad + 32]
                nc.vector.tensor_tensor(target.rearrange("p t (h d) -> p t h d", d=DK), o[:, :, :, 0:DK],
                                        rs[:, q, :, :].unsqueeze(3).broadcast_to([P, QT, 4, DK]),
                                        ALU.mult).then_inc(t1_read, 1)

            def residual(b):
                dve.wait_ge(t1_filled, uses_up_to(T1_ORDER, ("proj", b)))
                dve.wait_ge(folded, 3)
                t = slice(b * QT, (b + 1) * QT)
                nc.vector.scalar_tensor_tensor(x2[:, t, :], T1[:, 0:S].rearrange("p (t d) -> p t d", d=D),
                                               tg[:, 0:1], xg[:, t, :], ALU.mult, ALU.add).then_inc(t1_read, 1)
                dve.wait_ge(t1_read, reads_up_to(T1_ORDER, ("proj", b)))
                norm_stats(B + b, lambda t: x2[:, b * QT + t, :], b)

            def second_norm(b):
                normalise(B + b, h2, lambda t: x2[:, b * QT + t, :], b, h2_ready)

            def route_logits(b):
                dve.wait_ge(t1_filled, uses_up_to(T1_ORDER, ("router", b)))
                dve.wait_ge(ld_row, 16)
                nc.vector.scalar_tensor_tensor(rt[:, b, 0, :], T1[:, 0:E], 1.0 / S, br,
                                               ALU.mult, ALU.add).then_inc(t1_read, 1)
                dve.wait_ge(t1_read, reads_up_to(T1_ORDER, ("router", b)))
                link(nc.vector.reduce_max(sc[:, b, 0:1], rt[:, b, 0, :], axis=AX.X))
                nc.vector.tensor_scalar(rt[:, b, 1, :], rt[:, b, 0, :], sc[:, b, 0:1], None,
                                        ALU.subtract).then_inc(z_ready, 1)

            def route_top(b):
                dve.wait_ge(ez_ready, 2 * b + 1)
                link(nc.vector.reduce_sum(sc[:, b, 1:2], rt[:, b, 2, :], axis=AX.X))
                link(nc.vector.reciprocal(sc[:, b, 4:5], sc[:, b, 1:2]))
                link(nc.vector.tensor_scalar(rt[:, b, 3, :], rt[:, b, 2, :], sc[:, b, 4:5], None, ALU.mult))
                link(nc.vector.max(top[:, b, :], rt[:, b, 3, :]))
                nc.vector.tensor_tensor(sc[:, b, 2:3], top[:, b, 1:2], top[:, b, 0:1],
                                        ALU.subtract).then_inc(z_ready, 1)
                link(nc.vector.max_index(idx[:, b, :], top[:, b, :], rt[:, b, 3, :]))

            def route_shares(b):
                dve.wait_ge(ez_ready, 2 * b + 2)
                link(nc.vector.tensor_scalar(sc[:, b, 7:8], sc[:, b, 3:4], 1.0, None, ALU.add))
                link(nc.vector.reciprocal(sc[:, b, 5:6], sc[:, b, 7:8]))
                nc.vector.tensor_tensor(sc[:, b, 6:7], sc[:, b, 5:6], sc[:, b, 3:4], ALU.mult).then_inc(chosen, 1)
                dve.wait_ge(chosen, b + 1)

            def pick_up(b):
                dve.wait_ge(ld_w1, 16)
                dve.wait_ge(ld_col, 16)
                for s in range(2):
                    e = nc.vector.value_load(idx[0:1, b, s:s + 1], min_val=0, max_val=E - 1)
                    nc.vector.tensor_copy(b1e[:, b, s, :], col[:, bass.ds(e * FT, FT)]).then_inc(w1e_ready, 1)
                    nc.vector.tensor_copy(w1e[:, b, s, :], w1s[:, bass.ds(e * F, F)]).then_inc(w1e_ready, 1)
                    b2 = col[:, bass.ds(e + E * FT, 1)]
                    if s == 0:
                        link(nc.vector.tensor_scalar(b2e[:, b, 0:1], b2, sc[:, b, 5:6], None, ALU.mult))
                    else:
                        link(nc.vector.scalar_tensor_tensor(b2e[:, b, 1:2], b2, sc[:, b, 6:7], b2e[:, b, 0:1],
                                                            ALU.mult, ALU.add))

            def ffn_out(b):
                dve.wait_ge(down_done, b + 1)
                nc.vector.scalar_tensor_tensor(yT[:, b, :], downBank[b][:, 0:S], b2e[:, b, 1:2], h2T[:, b, :],
                                               ALU.add, ALU.add).then_inc(yT_ready, 1)

            def third_norm(b):
                dve.wait_ge(t0_filled, uses_up_to(T0_ORDER, ("yT", b)))
                norm_stats(2 * B + b, lambda t: T0[:, t * P:(t + 1) * P], b)

            def finish(b):
                n = 2 * B + b
                dve.wait_ge(rstd_ready, n + 1)
                for t in range(QT):
                    k = b * QT + t
                    nc.vector.tensor_scalar(yn[:, k, :], T0[:, t * P:(t + 1) * P], mv[:, n, t, 0:1],
                                            rstd[:, n, t:t + 1], ALU.subtract, ALU.mult).then_inc(t0_read, 1)
                    dve.wait_ge(t0_read, reads_before(T0_ORDER, ("yT", b)) + t + 1)
                    link(nc.vector.tensor_tensor(yg[:, k, :], yn[:, k, :], gam2[:, :], ALU.mult))
                    if t == 0:
                        dve.wait_ge(xo_ready, b + 1)
                    nc.vector.tensor_tensor(yo[:, k, :], yg[:, k, :], xo[:, k, :], ALU.add).then_inc(y_ready, 1)

            for k in range(CH):
                row_max(0, k)
            put_max(0)
            for i in range(UNITS):
                if i + 1 < UNITS:
                    row_max(i + 1, 0)
                qB_copy(i)
                if i + 1 < UNITS:
                    for k in range(1, CH):
                        row_max(i + 1, k)
                small = SMALL_IN.get(i)
                if small and small[0] == "O":
                    o_norm(small[1])
                elif small == ("proj", 0):
                    residual(0)
                if i + 1 < UNITS:
                    put_max(i + 1)
                if small == ("O", 5):
                    second_norm(0)
            route_logits(0)
            o_norm(6)
            route_top(0)
            route_shares(0)
            pick_up(0)
            o_norm(7)
            residual(1)
            second_norm(1)
            route_logits(1)
            route_top(1)
            route_shares(1)
            pick_up(1)
            ffn_out(0)
            third_norm(0)
            finish(0)
            ffn_out(1)
            third_norm(1)
            finish(1)

        @block.tensor
        def _(pe):
            def kv_project(n):
                if n == 0:
                    pe.wait_ge(ld_w, 16)
                    pe.wait_ge(ld_c0, 16)
                if n == 2:
                    pe.wait_ge(ld_c1, 16)
                bank = bankA[n] if n < 2 else bankB[n - 2]
                for t in range(2):
                    last = nc.tensor.matmul(bank[:, t * 2 * D:(t + 1) * 2 * D],
                                            cT[:, (2 * n + t) * P:(2 * n + t + 1) * P], w[:, 0:2 * D],
                                            start=True, stop=True)
                last.then_inc(kvp_done, 1)

            def transposes(bank, sources, identity, done):
                for t, source in enumerate(sources):
                    last = nc.tensor.transpose(bank[:, t * P:(t + 1) * P], source, identity[:, :])
                last.then_inc(done, 1)

            def h_transpose(b):
                pe.wait_ge(ident_ready, 1)
                pe.wait_ge(h_ready, QT * (b + 1))
                bank, filled = (T1, t1_filled) if b == 0 else (T0, t0_filled)
                transposes(bank, [h[:, b * QT + t, :] for t in range(QT)], ident, filled)

            def q_project(b):
                bank, read = (bankA[2], t1_read) if b == 0 else (bankV, t0_read)
                pe.wait_ge(read, 1)
                for t in range(QT):
                    last = nc.tensor.matmul(bank[:, t * D:(t + 1) * D],
                                            hT[:, b * S + t * P:b * S + (t + 1) * P], w[:, 2 * D:3 * D],
                                            start=True, stop=True)
                last.then_inc(qp_done, 1)

            def stack(i):
                b, g = divmod(i, UPB)
                if i == 0:
                    pe.wait_ge(pads_ready, 2)
                    pe.wait_ge(qpads_ready, 1)
                if g == 0:
                    pe.wait_ge(kpart[b], 4)
                    pe.wait_ge(qpart[b], 4)
                pe.wait_ge(t0_read, reads_before(T0_ORDER, ("stack", i)))
                transposes(T0b, [kst[:, b * KT + t, g, :] for t in range(KT)]
                           + [qst[:, b * QT + t, g, :] for t in range(QT)], identb, t0_filled)

            def scores_a(i, k):
                c = CH * i + k
                j, t = divmod(k, QT)
                if k == 0:
                    pe.wait_ge(t0_read, reads_up_to(T0_ORDER, ("stack", i)))
                if c == 0:
                    pe.wait_ge(kf_ready, 2)
                    pe.wait_ge(vx_ready, 4)
                    pe.wait_ge(qf_ready, 1)
                if c >= 3:
                    pe.wait_ge(a_read, c - 2)
                nc.tensor.matmul(bankA[c % 3][:, :], qA[:, i % RING, j, t * P:(t + 1) * P], kT[:, i, :],
                                 start=True, stop=True).then_inc(a_filled, 1)

            def max_stack(i):
                b, g = divmod(i, UPB)
                pe.wait_ge(m_ready, i + 1)
                pe.wait_ge(t1_read, reads_before(T1_ORDER, ("max", i)))
                transposes(T1b, [qst[:, b * QT + t, g, :] for t in range(QT)], identb, t1_filled)

            def scores_b(i, k):
                c = CH * i + k
                j, half_ = divmod(k, 2)
                if k == 0:
                    pe.wait_ge(t1_read, reads_up_to(T1_ORDER, ("max", i)))
                if c == 0:
                    pe.wait_ge(kf_ready, 4)
                    pe.wait_ge(vx_ready, 8)
                if c >= 2:
                    pe.wait_ge(p_ready, c - 1)
                for t in range(2):
                    kt = 2 * half_ + t
                    last = nc.tensor.matmul(bankB[c % 2][:, t * S:(t + 1) * S],
                                            kT[j * HB:(j + 1) * HB, i, kt * P:(kt + 1) * P],
                                            qB[j * HB:(j + 1) * HB, i % RING, :], start=True, stop=True)
                last.then_inc(b_filled, 1)

            def values(q, kt):
                b, quad = divmod(q, QUADS // B)
                pe.wait_ge(p_ready, CH * (2 * q + 1) + 2 + kt // 2 + 1)
                if kt == 0:
                    if q == 0:
                        pe.wait_ge(qf_ready, 2)
                    else:
                        pe.wait_ge(oT_ready, q)
                for n in range(4):
                    last = nc.tensor.matmul(bankV[32 * n:32 * n + 32, 0:S], vx[:, b * KT + kt, 4 * quad + n, :],
                                            pr[:, q % 2, n, kt, :], start=(kt == 0), stop=(kt == KT - 1))
                if kt == KT - 1:
                    last.then_inc(pv_done, 1)

            def small(name):
                what, n = name
                pe.wait_ge(t1_read, reads_before(T1_ORDER, name))
                tokens = range(n * QT, (n + 1) * QT)
                if what == "O":
                    pe.wait_ge(oT_ready, n + 1)
                    transposes(T1, [oT[:, n % 2, t * P:(t + 1) * P] for t in range(QT)], ident, t1_filled)
                elif what == "attnT":
                    transposes(T1, [attn[:, t, :] for t in tokens], ident, t1_filled)
                elif what == "proj":
                    for t in range(QT):
                        last = nc.tensor.matmul(T1[:, t * D:(t + 1) * D], attnT[:, n, t * P:(t + 1) * P],
                                                w[:, 3 * D:4 * D], start=True, stop=True)
                    last.then_inc(t1_filled, 1)
                elif what == "h2T":
                    pe.wait_ge(h2_ready, QT * (n + 1))
                    transposes(T1, [h2[:, t, :] for t in tokens], ident, t1_filled)
                else:
                    pe.wait_ge(ld_col, 16)
                    nc.tensor.matmul(T1[:, 0:E], hsum[:, n:n + 1].broadcast_to([P, P]),
                                     col[:, E * FT + E:COLS], start=True, stop=True).then_inc(t1_filled, 1)

            def up(b, n):
                if n % FT == 0:
                    pe.wait_ge(w1e_ready, 4 * b + 2 * (n // FT + 1))
                before = 2 * FT * b + n - 4
                if before < 0:
                    pe.wait_ge(a_read, CH * UNITS)
                    pe.wait_ge(p_ready, CH * UNITS)
                else:
                    pe.wait_ge(hid_ready, before + 1)
                nc.tensor.matmul(upBank[n % 4][:, 0:S], w1e[:, b, n // FT, (n % FT) * P:(n % FT + 1) * P],
                                 h2T[:, b, :], start=True, stop=True).then_inc(up_done, 1)

            def down(b, n):
                if n % FT == 0:
                    pe.wait_ge(w2e_ready, 2 * b + n // FT + 1)
                if b == 1 and n == 0:
                    pe.wait_ge(oT_ready, QUADS)
                pe.wait_ge(hid_ready, 2 * FT * b + n + 1)
                last = nc.tensor.matmul(downBank[b][:, 0:S], w2e[:, b, n // FT, (n % FT) * P:(n % FT + 1) * P],
                                        hid[:, b, n, :], start=(n == 0), stop=(n == 2 * FT - 1))
                if n == 2 * FT - 1:
                    last.then_inc(down_done, 1)

            def y_transpose(b):
                pe.wait_ge(yT_ready, b + 1)
                pe.wait_ge(t0_read, reads_before(T0_ORDER, ("yT", b)))
                transposes(T0, [yT[:, b, t * P:(t + 1) * P] for t in range(QT)], ident, t0_filled)

            kv_project(0)
            kv_project(1)
            h_transpose(0)
            q_project(0)
            h_transpose(1)
            kv_project(2)
            kv_project(3)
            q_project(1)
            for i in range(RING):
                stack(i)
            for k in range(CH):
                scores_a(0, k)
            scores_a(1, 0)
            scores_a(1, 1)
            for i in range(UNITS):
                q, r = (i - 2) // 2, 2 * (i % 2)
                if i + 1 < UNITS:
                    scores_a(i + 1, 2)
                max_stack(i)
                if q >= 0:
                    values(q, r)
                if i + 1 < UNITS:
                    scores_a(i + 1, 3)
                scores_b(i, 0)
                scores_b(i, 1)
                if q >= 0:
                    values(q, r + 1)
                if i in SMALL_IN:
                    small(SMALL_IN[i])
                if i + 2 < UNITS:
                    scores_a(i + 2, 0)
                scores_b(i, 2)
                if i + 2 < UNITS:
                    scores_a(i + 2, 1)
                scores_b(i, 3)
                if i + RING < UNITS:
                    stack(i + RING)
            small(("router", 0))
            small(("O", 6))
            for kt in range(KT):
                values(QUADS - 1, kt)
            between = {0: ("O", 7), 1: ("attnT", 1), 3: ("proj", 1), 5: ("h2T", 1), 7: ("router", 1)}
            for b in range(B):
                for n in range(2 * FT + 2):
                    if n < 2 * FT:
                        up(b, n)
                    if n >= 2:
                        down(b, n - 2)
                    if b == 0 and n in between:
                        small(between[n])
                y_transpose(b)


_OUT = "out_dram"


def kernel(**inputs):
    import numpy as np
    import concourse.bacc as bacc
    from concourse.bass_utils import run_bass_kernel_spmd

    a = {k: np.asarray(v) for k, v in inputs.items()}
    xa, ff = "L0_xattn_", "L0_ffn_"
    arrays = {
        "x_in": a["x"].reshape(B * QT, P, D).transpose(1, 0, 2).reshape(P, B * QT * D),
        "ctx_in": a["ctx_1024"].reshape(B * C, D).T,
        "w_in": np.concatenate([a[xa + n].T for n in ("Wk", "Wv", "Wq", "Wo")], axis=1),
        "w1_in": a[ff + "W1"].transpose(1, 0, 2).reshape(P, E * F),
        "w2_in": a[ff + "W2"].reshape(E, FT, P, D).transpose(2, 0, 1, 3).reshape(P, E * F),
        "cols_in": np.concatenate([a[ff + "b1"].reshape(E * FT, P).T, a[ff + "b2"].T, a[ff + "Wr"]], axis=1),
        "rows_in": np.concatenate([a[xa + "bq"], a[xa + "bk"], a[xa + "bv"], a[xa + "bo"], a[ff + "gamma"],
                                   a[ff + "beta"], a[ff + "br"], a["g_xattn"], a["g_ffn"]]),
    }
    arrays = {k: np.ascontiguousarray(v) for k, v in arrays.items()}
    nc = bacc.Bacc("TRN2", target_bir_lowering=False, num_devices=1)
    args = [nc.dram_tensor(k, v.shape, mybir.dt.from_np(v.dtype), kind="ExternalInput").ap()
            for k, v in arrays.items()]
    out = nc.dram_tensor(_OUT, (B * S, D), mybir.dt.float32, kind="ExternalOutput").ap()
    build(nc, *args, out)
    r = run_bass_kernel_spmd(nc, [arrays], core_ids=[0])
    return r.results[0][_OUT].reshape(B, S, D)
```

```python
import concourse.bass as bass
from concourse import mybir
from contextlib import ExitStack
import math

B, S, C, D = 2, 256, 512, 128
H, DK = 16, 8
E, F = 8, 512
P = 128
QT, KT = S // P, C // P
FT = F // P
UNITS = B * H // 2
UPB = UNITS // B
QUADS = UNITS // 2
HB = 64
MAXROW = 48
CH = 4
RING = 3
SCALE = 1.0 / math.sqrt(DK)
EPS = 1e-5
ROWS = 6 * D + E + 2
COLS = E * FT + E + E

SMALL_IN = {4: ("O", 0), 6: ("O", 1), 8: ("O", 2), 10: ("O", 3), 11: ("attnT", 0), 12: ("proj", 0),
            13: ("O", 4), 14: ("h2T", 0), 15: ("router", 0)}
T0_ORDER = [("hT", 1)] + [("stack", _i) for _i in range(RING)]
for _i in range(UNITS):
    T0_ORDER += [SMALL_IN[_i]] if _i in SMALL_IN else []
    T0_ORDER += [("stack", _i + RING)] if _i + RING < UNITS else []
T0_ORDER += [("O", 5), ("O", 6), ("O", 7), ("attnT", 1), ("proj", 1), ("h2T", 1), ("router", 1)]
T1_ORDER = [("hT", 0)] + [("max", _i) for _i in range(UNITS)] + [("yT", 0), ("yT", 1)]
READERS = {"stack": 3, "yT": 2}


def uses_up_to(order, name):
    return order.index(name) + 1


def reads_before(order, name):
    return sum(READERS.get(n, 1) for n, _ in order[:order.index(name)])


def reads_up_to(order, name):
    return reads_before(order, name) + READERS.get(name[0], 1)


def build(nc, x, ctxT, wqkvo, w1, w2, cols, rows, out):
    f32, bf16, u32 = mybir.dt.float32, mybir.dt.bfloat16, mybir.dt.uint32
    ALU, ACT, AX = mybir.AluOpType, mybir.ActivationFunctionType, mybir.AxisListType
    ctx = ExitStack()
    with ctx:
        def sb(name, shape, dt=f32):
            return ctx.enter_context(nc.sbuf_tensor(name, shape, dt))

        def ps(name, shape, dt=f32):
            return ctx.enter_context(nc.psum_tensor(name, shape, dt))

        def sem(name):
            return ctx.enter_context(nc.semaphore(name))

        xs = sb("xs", [P, B * QT, D])
        cT = sb("cT", [P, B * KT * P])
        w = sb("w", [P, 4 * D])
        w1s = sb("w1s", [P, E * F])
        w2s = sb("w2s", [P, E * F])
        col = sb("col", [P, COLS])
        row = sb("row", [P, ROWS])
        bk, bv, bq, bo, gamma, beta = (row[:, n * D:(n + 1) * D] for n in (1, 2, 0, 3, 4, 5))
        br = row[:, 6 * D:6 * D + E]
        gates = row[:, 6 * D + E:ROWS]
        ident = sb("ident", [P, P])
        identb = sb("identb", [P, P], bf16)
        tg = sb("tg", [P, 2])
        xg = sb("xg", [P, B * QT, D])
        gam2 = sb("gam2", [P, D])
        bet2 = sb("bet2", [P, D])
        half = sb("half", [P, QT])
        euler = sb("euler", [P, E])
        LN = 3 * B
        stats = sb("stats", [P, LN, QT, 6])
        mv = sb("mv", [P, LN, QT, 2])
        veps = sb("veps", [P, LN, QT])
        rstd = sb("rstd", [P, LN, QT])
        h = sb("h", [P, B * QT, D])
        hT = sb("hT", [P, B * S])
        qf = sb("qf", [P, B * QT, D])
        qr = sb("qr", [P, B * QT, D])
        kf = sb("kf", [P, B * KT, D])
        kr = sb("kr", [P, B * KT, D])
        qst = sb("qst", [P, B * QT, H // 2, P], bf16)
        kst = sb("kst", [P, B * KT, H // 2, P], bf16)
        kT = sb("kT", [P, UNITS, C], bf16)
        qA = sb("qA", [P, RING, 2, S], bf16)
        qB = sb("qB", [P, RING, S], bf16)
        vx = sb("vx", [P, B * KT, H, 32])
        nmax = sb("nmax", [P, UNITS, CH])
        pr = sb("pr", [P, 2, 4, KT, S])
        oT = sb("oT", [P, 2, S])
        rs = sb("rs", [P, QUADS, QT, 4])
        attn = sb("attn", [P, B * QT, D])
        attnT = sb("attnT", [P, B, S])
        tbo = sb("tbo", [P, D])
        x2 = sb("x2", [P, B * QT, D])
        xo = sb("xo", [P, B * QT, D])
        h2 = sb("h2", [P, B * QT, D])
        h2T = sb("h2T", [P, B, S])
        hsum = sb("hsum", [P, B])
        rt = sb("rt", [P, B, 8, E])
        top = sb("top", [P, B, E])
        idx = sb("idx", [P, B, E], u32)
        sc = sb("sc", [P, B, 16])
        w1e = sb("w1e", [P, B, 2, F])
        w2e = sb("w2e", [P, B, 2, F])
        b1e = sb("b1e", [P, B, 2, FT])
        b2e = sb("b2e", [P, B, 2])
        hid = pr[:, 0, :, :, :].rearrange("p h k s -> p (h k) s").rearrange("p (b n) s -> p b n s", b=B)
        yT = sb("yT", [P, B, S])
        yg = sb("yg", [P, B * QT, D])
        yo = sb("yo", [P, B * QT, D])

        bankA = [ps(f"bankA{n}", [P, 512]) for n in range(3)]
        bankB = [ps(f"bankB{n}", [P, 512]) for n in range(2)]
        bankV = ps("bankV", [P, 512])
        T0 = ps("T0", [P, 512])
        T1 = ps("T1", [P, 512])
        T0b = T0[:, :].bitcast(bf16)
        T1b = T1[:, :].bitcast(bf16)

        ld_x, ld_w, ld_row, ld_c0, ld_c1 = sem("ld_x"), sem("ld_w"), sem("ld_row"), sem("ld_c0"), sem("ld_c1")
        ld_col, ld_w1, ld_w2 = sem("ld_col"), sem("ld_w1"), sem("ld_w2")
        stored = sem("stored")
        ident_ready = sem("ident_ready")
        consts_ready = sem("consts_ready")
        pads_ready = sem("pads_ready")
        tanh_ready = sem("tanh_ready")
        folded = sem("folded")
        veps_ready, rstd_ready = sem("veps_ready"), sem("rstd_ready")
        h_ready = sem("h_ready")
        qp_done, kvp_done = sem("qp_done"), sem("kvp_done")
        qf_ready, kf_ready, vx_ready = sem("qf_ready"), sem("kf_ready"), sem("vx_ready")
        kpart = [sem(f"kpart{b}") for b in range(B)]
        qpart = [sem(f"qpart{b}") for b in range(B)]
        t0_filled, t0_read = sem("t0_filled"), sem("t0_read")
        t1_filled, t1_read = sem("t1_filled"), sem("t1_read")
        a_filled, a_read = sem("a_filled"), sem("a_read")
        m_high, m_ready = sem("m_high"), sem("m_ready")
        qmask_ready = sem("qmask_ready")
        qpads_ready = sem("qpads_ready")
        b_filled, p_ready = sem("b_filled"), sem("p_ready")
        pv_done, oT_ready = sem("pv_done"), sem("oT_ready")
        rs_ready = sem("rs_ready")
        h2_ready = sem("h2_ready")
        xo_ready = sem("xo_ready")
        z_ready, ez_ready = sem("z_ready"), sem("ez_ready")
        chosen = sem("chosen")
        w1e_ready, w2e_ready = sem("w1e_ready"), sem("w2e_ready")
        up_done, hid_ready, down_done = sem("up_done"), sem("hid_ready"), sem("down_done")
        yT_ready = sem("yT_ready")
        y_ready = sem("y_ready")
        chain = sem("chain")
        pchain = sem("pchain")

        upBank = [bankA[0], bankA[1], bankA[2], bankB[1]]
        downBank = [bankB[0], bankV]

        kst_blocks = kst[:, :, :, :].rearrange("p t g (j c) -> p (t g j) c", c=HB)
        qst_blocks = qst[:, :, :, :].rearrange("p t g (j c) -> p (t g j) c", c=HB)

        def heads(t, b, tiles):
            return t[:, b * tiles:(b + 1) * tiles, :].rearrange("p t (h d) -> p (t h) d", d=DK)

        def slots(blocks, b, tiles, first, step, count):
            part = blocks[:, b * tiles * H:(b + 1) * tiles * H, 0:MAXROW].rearrange("p n (s d) -> p n s d", d=DK)
            return part[:, :, first:first + step * (count - 1) + 1:step, :]

        def over(a, count):
            return a.unsqueeze(2).broadcast_to([P, a.shape[1], count, DK])

        QPARTS = [(0, 1, 3), (3, 2, 2), (4, 1, 1)]
        KPARTS = [(2, 1, 3), (1, 4, 2), (0, 1, 1)]

        def cut(step, copy, sub, blocks, full, rest, b, tiles, parts):
            high = slots(blocks, b, tiles, *parts[0])
            mid = slots(blocks, b, tiles, *parts[1])
            low = slots(blocks, b, tiles, *parts[2])
            v, r = heads(full, b, tiles), heads(rest, b, tiles)
            if step == 0:
                return copy(high, over(v, 3))
            if step == 1:
                return sub(r, v, high[:, :, 0, :])
            if step == 2:
                return copy(mid, over(r, 2))
            return sub(low[:, :, 0, :], r, mid[:, :, 0, :])

        block = ctx.enter_context(nc.Block())

        @block.sync
        def _(sp):
            sp.dma_start(xs[:, :, :], x.rearrange("p (t d) -> p t d", d=D)).then_inc(ld_x, 16)
            sp.dma_start(cT[:, 0:C], ctxT[:, 0:C]).then_inc(ld_c0, 16)
            sp.dma_start(cT[:, C:2 * C], ctxT[:, C:2 * C]).then_inc(ld_c1, 16)
            sp.dma_start(col[:, :], cols).then_inc(ld_col, 16)
            sp.dma_start(w1s[:, :], w1).then_inc(ld_w1, 16)
            sp.dma_start(w2s[:, :], w2).then_inc(ld_w2, 16)
            for b in range(B):
                for t in range(QT):
                    n = b * QT + t
                    sp.wait_ge(y_ready, n + 1)
                    sp.dma_start(out[n * P:(n + 1) * P, :], yo[:, n, :]).then_inc(stored, 16)
            sp.wait_ge(stored, 16 * B * QT)

        @block.gpsimd
        def _(pool):
            steps = [0]

            def link(ins):
                steps[0] += 1
                ins.then_inc(pchain, 1)
                pool.wait_ge(pchain, steps[0])

            pool.memset(half[:, :], -0.5).then_inc(consts_ready, 1)
            link(pool.memset(ident[:, :], 0.0))
            link(pool.affine_select(out=ident[:, :], in_=ident[:, :], compare_op=ALU.not_equal, fill=1.0,
                                    base=0, pattern=[[-1, P]], channel_multiplier=1))
            pool.tensor_copy(identb[:, :], ident[:, :]).then_inc(ident_ready, 1)
            pool.memset(kst_blocks[:, :, MAXROW:MAXROW + 2], 1.0).then_inc(pads_ready, 1)
            pool.memset(kst_blocks[:, :, MAXROW + 2:HB], 0.0).then_inc(pads_ready, 1)
            pool.memset(euler[:, :], math.e).then_inc(consts_ready, 1)

            def power(base, exponent, result, done):
                pool.tensor_tensor(result, base, exponent, ALU.pow).then_inc(done, 1)

            pool.wait_ge(consts_ready, 2)
            for b in range(B):
                pool.wait_ge(veps_ready, b + 1)
                power(veps[:, b, :], half[:, :], rstd[:, b, :], rstd_ready)
            pool.memset(vx[:, :, :, DK:DK + 1], 1.0).then_inc(pads_ready, 1)
            pool.memset(vx[:, :, :, DK + 1:32], 0.0).then_inc(pads_ready, 1)
            pool.wait_ge(ld_row, 16)
            pool.wait_ge(tanh_ready, 1)
            pool.wait_ge(ld_x, 16)
            pool.tensor_scalar(gam2[:, :], gamma, tg[:, 1:2], None, ALU.mult).then_inc(folded, 1)
            pool.tensor_scalar(bet2[:, :], beta, tg[:, 1:2], None, ALU.mult).then_inc(folded, 1)
            link(pool.tensor_scalar(tbo[:, :], bo, tg[:, 0:1], None, ALU.mult))
            pool.tensor_tensor(xg[:, :, :], xs[:, :, :], tbo[:, :].unsqueeze(1).broadcast_to([P, B * QT, D]),
                               ALU.add).then_inc(folded, 1)
            for full, rest, blocks, tiles, parts, ready, part in (
                    (qf, qr, qst_blocks, QT, QPARTS, qf_ready, qpart[1]),
                    (kf, kr, kst_blocks, KT, KPARTS, kf_ready, kpart[1])):
                pool.wait_ge(ready, 2 if tiles == QT else 4)
                for s in range(4):
                    if s:
                        pool.wait_ge(part, s)
                    cut(s, pool.tensor_copy,
                        lambda o, a, c: pool.tensor_tensor(o, a, c, ALU.subtract),
                        blocks, full, rest, 1, tiles, parts).then_inc(part, 1)
            def router_powers(b):
                pool.wait_ge(z_ready, 2 * b + 1)
                power(euler[:, :], rt[:, b, 1, :], rt[:, b, 2, :], ez_ready)
                pool.wait_ge(z_ready, 2 * b + 2)
                power(euler[:, 0:1], sc[:, b, 2:3], sc[:, b, 3:4], ez_ready)

            def norm_power(n):
                pool.wait_ge(veps_ready, n + 1)
                power(veps[:, n, :], half[:, :], rstd[:, n, :], rstd_ready)

            def output_base(b):
                pool.wait_ge(t0_read, reads_up_to(T0_ORDER, ("proj", b)))
                pool.wait_ge(folded, 3)
                pool.tensor_tensor(xo[:, b * QT:(b + 1) * QT, :], x2[:, b * QT:(b + 1) * QT, :],
                                   bet2[:, :].unsqueeze(1).broadcast_to([P, QT, D]), ALU.add).then_inc(xo_ready, 1)

            norm_power(B)
            output_base(0)
            router_powers(0)
            norm_power(B + 1)
            output_base(1)
            router_powers(1)
            norm_power(2 * B)
            norm_power(2 * B + 1)

        @block.scalar
        def _(act):
            def act_copy(o, a):
                return nc.scalar.activation(o, a, ACT.Copy)

            act.dma_start(w[:, :], wqkvo).then_inc(ld_w, 16)
            act.dma_start(row[:, :], rows.partition_broadcast(P)).then_inc(ld_row, 16)
            act.wait_ge(ld_row, 16)
            nc.scalar.activation(tg[:, :], gates, ACT.Tanh).then_inc(tanh_ready, 1)
            for b in range(B):
                bank, filled, read, use = (T1, t1_filled, t1_read, 1) if b == 0 else (T0, t0_filled, t0_read, 1)
                act.wait_ge(filled, use)
                act_copy(hT[:, b * S:(b + 1) * S], bank[:, 0:S]).then_inc(read, 1)
            for s in (0, 2):
                for full, rest, blocks, tiles, parts, ready, part, count in (
                        (qf, qr, qst_blocks, QT, QPARTS, qf_ready, qpart[0], 1),
                        (kf, kr, kst_blocks, KT, KPARTS, kf_ready, kpart[0], 2)):
                    act.wait_ge(ready, count)
                    if s:
                        act.wait_ge(part, s)
                    cut(s, act_copy, None, blocks, full, rest, 0, tiles, parts).then_inc(part, 1)

            def stack_copy(i):
                act.wait_ge(t0_filled, uses_up_to(T0_ORDER, ("stack", i)))
                act_copy(kT[:, i, :], T0b[:, 0:C]).then_inc(t0_read, 1)
                if i >= RING:
                    act.wait_ge(a_filled, CH * (i - RING + 1))
                if i == 0:
                    act.wait_ge(qmask_ready, 1)
                for j in range(2):
                    act_copy(qA[j * HB:(j + 1) * HB, i % RING, j, :],
                             T0b[j * HB:(j + 1) * HB, C:C + S]).then_inc(t0_read, 1)

            def exps(i, k):
                q, j, half_ = i // 2, k // 2, k % 2
                act.wait_ge(b_filled, CH * i + k + 1)
                if q >= 2:
                    act.wait_ge(pv_done, q - 1)
                nc.scalar.activation(
                    pr[:, q % 2, (i % 2) * 2 + j, 2 * half_:2 * half_ + 2, :],
                    bankB[k % 2][:, :].rearrange("p (t s) -> p t s", t=2),
                    ACT.Exp, scale=SCALE).then_inc(p_ready, 1)

            def o_copy(q):
                act.wait_ge(pv_done, q + 1)
                if q >= 2:
                    act.wait_ge(t0_filled, uses_up_to(T0_ORDER, ("O", q - 2)))
                act_copy(oT[:, q % 2, :], bankV[:, 0:S]).then_inc(oT_ready, 1)

            def attnT_copy(b):
                act.wait_ge(t0_filled, uses_up_to(T0_ORDER, ("attnT", b)))
                act_copy(attnT[:, b, :], T0[:, 0:S]).then_inc(t0_read, 1)

            def h2T_copy(b):
                act.wait_ge(t0_filled, uses_up_to(T0_ORDER, ("h2T", b)))
                nc.scalar.activation(h2T[:, b, :], T0[:, 0:S], ACT.Copy,
                                     accum_out=hsum[:, b:b + 1]).then_inc(t0_read, 1)

            def pick_down(b, s):
                act.wait_ge(chosen, b + 1)
                act.wait_ge(ld_w2, 16)
                e = nc.scalar.value_load(idx[0:1, b, s:s + 1], min_val=0, max_val=E - 1)
                nc.scalar.activation(w2e[:, b, s, :], w2s[:, bass.ds(e * F, F)], ACT.Copy,
                                     scale=sc[:, b, 5 + s:6 + s]).then_inc(w2e_ready, 1)

            def gelu(b, n):
                act.wait_ge(up_done, 2 * FT * b + n + 1)
                nc.scalar.activation(hid[:, b, n, :], upBank[n % 4][:, 0:S], ACT.Gelu,
                                     bias=b1e[:, b, n // FT, n % FT:n % FT + 1]).then_inc(hid_ready, 1)

            for i in range(RING):
                stack_copy(i)
            for i in range(UNITS):
                exps(i, 0)
                exps(i, 1)
                if SMALL_IN.get(i) == ("attnT", 0):
                    attnT_copy(0)
                if SMALL_IN.get(i) == ("h2T", 0):
                    h2T_copy(0)
                exps(i, 2)
                if i == UNITS - 1:
                    o_copy(6)
                exps(i, 3)
                if i >= 3 and i % 2 == 1 and i < UNITS - 1:
                    o_copy((i - 3) // 2)
                if i + RING < UNITS:
                    stack_copy(i + RING)
            o_copy(7)
            pick_down(0, 0)
            attnT_copy(1)
            pick_down(0, 1)
            for n in range(FT):
                gelu(0, n)
            h2T_copy(1)
            for n in range(FT, 2 * FT):
                gelu(0, n)
            pick_down(1, 0)
            for n in range(FT):
                gelu(1, n)
            pick_down(1, 1)
            for n in range(FT, 2 * FT):
                gelu(1, n)

        @block.vector
        def _(dve):
            steps = [0]

            def link(ins):
                steps[0] += 1
                ins.then_inc(chain, 1)
                dve.wait_ge(chain, steps[0])

            def norm_stats(n, source, b):
                for t in range(QT):
                    last = nc.vector.bn_stats(stats[:, n, t, :], source(t))
                    if t == QT - 1:
                        link(last)
                    else:
                        steps[0] += 1
                        last.then_inc(chain, 1)
                for t in range(QT):
                    last = nc.vector.bn_aggr(mv[:, n, t, :], stats[:, n, t, :])
                    if t == QT - 1:
                        link(last)
                    else:
                        steps[0] += 1
                        last.then_inc(chain, 1)
                nc.vector.tensor_scalar(veps[:, n, :], mv[:, n, :, 1], EPS, None, ALU.add).then_inc(veps_ready, 1)

            def normalise(n, target, source, b, done):
                dve.wait_ge(rstd_ready, n + 1)
                for t in range(QT):
                    nc.vector.tensor_scalar(target[:, b * QT + t, :], source(t), mv[:, n, t, 0:1],
                                            rstd[:, n, t:t + 1], ALU.subtract, ALU.mult).then_inc(done, 1)

            nc.vector.memset(qA[:, :, :, :].rearrange("p r j s -> p (r j s)").bitcast(u32), 0).then_inc(qmask_ready, 1)
            nc.vector.memset(qst_blocks[:, :, MAXROW:HB], 0.0).then_inc(qpads_ready, 1)
            dve.wait_ge(ld_x, 16)
            for b in range(B):
                norm_stats(b, lambda t: xs[:, b * QT + t, :], b)
            for b in range(B):
                normalise(b, h, lambda t: xs[:, b * QT + t, :], b, h_ready)

            def q_bias(b):
                dve.wait_ge(qp_done, b + 1)
                bank = bankA[2] if b == 0 else bankV
                nc.vector.tensor_tensor(qf[:, b * QT:(b + 1) * QT, :],
                                        bank[:, 0:S].rearrange("p (t d) -> p t d", d=D),
                                        bq.unsqueeze(1).broadcast_to([P, QT, D]), ALU.add).then_inc(qf_ready, 1)

            def kv_view(n):
                bank = bankA[n] if n < 2 else bankB[n - 2]
                return bank[:, :].rearrange("p (t d) -> p t d", d=2 * D)

            def k_bias(n):
                dve.wait_ge(kvp_done, n + 1)
                nc.vector.tensor_tensor(kf[:, 2 * n:2 * n + 2, :], kv_view(n)[:, :, 0:D],
                                        bk.unsqueeze(1).broadcast_to([P, 2, D]), ALU.add).then_inc(kf_ready, 1)

            def v_bias(n):
                if n == 0:
                    dve.wait_ge(pads_ready, 4)
                for t in range(2):
                    nc.vector.tensor_tensor(vx[:, 2 * n + t, :, 0:DK],
                                            kv_view(n)[:, t, D:2 * D].rearrange("p (h d) -> p h d", d=DK),
                                            bv.rearrange("p (h d) -> p h d", d=DK), ALU.add).then_inc(vx_ready, 1)

            dve.wait_ge(ld_row, 16)
            q_bias(0)
            k_bias(0)
            k_bias(1)
            sub = lambda o, a, c: nc.vector.tensor_tensor(o, a, c, ALU.subtract)
            for s in (1, 3):
                for full, rest, blocks, tiles, parts, part, ready, n in (
                        (qf, qr, qst_blocks, QT, QPARTS, qpart[0], qf_ready, 1),
                        (kf, kr, kst_blocks, KT, KPARTS, kpart[0], kf_ready, 2)):
                    dve.wait_ge(part, s)
                    cut(s, None, sub, blocks, full, rest, 0, tiles, parts).then_inc(part, 1)
                if s == 1:
                    v_bias(0)
                    v_bias(1)
            q_bias(1)
            k_bias(2)
            k_bias(3)
            v_bias(2)
            v_bias(3)

            def row_max(i, k):
                c = CH * i + k
                dve.wait_ge(a_filled, c + 1)
                nc.vector.reduce_max(nmax[:, i, k:k + 1], bankA[c % 3][:, :], axis=AX.X,
                                     negate=True).then_inc(a_read, 1)

            def max_columns(i):
                b, g = divmod(i, UPB)
                return (qst[:, b * QT:(b + 1) * QT, g, :].rearrange("p t (j c) -> p j t c", c=HB),
                        nmax[:, i, :].rearrange("p (j t) -> p j t", j=2))

            def max_high(i):
                columns, m = max_columns(i)
                dve.wait_ge(a_read, CH * (i + 1))
                nc.vector.tensor_copy(columns[:, :, :, MAXROW], m).then_inc(m_high, 1)

            def max_low(i):
                columns, m = max_columns(i)
                dve.wait_ge(m_high, i + 1)
                nc.vector.tensor_tensor(columns[:, :, :, MAXROW + 1], m, columns[:, :, :, MAXROW],
                                        ALU.subtract).then_inc(m_ready, 1)

            def qB_copy(i):
                dve.wait_ge(t1_filled, uses_up_to(T1_ORDER, ("max", i)))
                if i >= RING:
                    dve.wait_ge(b_filled, CH * (i - RING + 1))
                nc.vector.tensor_copy(qB[:, i % RING, :], T1b[:, 0:S]).then_inc(t1_read, 1)

            def o_sums(q):
                dve.wait_ge(t0_filled, uses_up_to(T0_ORDER, ("O", q)))
                o = T0[:, 0:S].rearrange("p (t h c) -> p t h c", t=QT, h=4)
                nc.vector.reciprocal(rs[:, q, :, :], o[:, :, :, DK]).then_inc(rs_ready, 1)

            def o_norm(q):
                b, quad = divmod(q, QUADS // B)
                o = T0[:, 0:S].rearrange("p (t h c) -> p t h c", t=QT, h=4)
                dve.wait_ge(rs_ready, q + 1)
                target = attn[:, b * QT:(b + 1) * QT, 32 * quad:32 * quad + 32]
                nc.vector.tensor_tensor(target.rearrange("p t (h d) -> p t h d", d=DK), o[:, :, :, 0:DK],
                                        rs[:, q, :, :].unsqueeze(3).broadcast_to([P, QT, 4, DK]),
                                        ALU.mult).then_inc(t0_read, 1)

            def residual(b):
                dve.wait_ge(t0_filled, uses_up_to(T0_ORDER, ("proj", b)))
                dve.wait_ge(folded, 3)
                t = slice(b * QT, (b + 1) * QT)
                nc.vector.scalar_tensor_tensor(x2[:, t, :], T0[:, 0:S].rearrange("p (t d) -> p t d", d=D),
                                               tg[:, 0:1], xg[:, t, :], ALU.mult, ALU.add).then_inc(t0_read, 1)
                dve.wait_ge(t0_read, reads_up_to(T0_ORDER, ("proj", b)))
                norm_stats(B + b, lambda t: x2[:, b * QT + t, :], b)

            def second_norm(b):
                normalise(B + b, h2, lambda t: x2[:, b * QT + t, :], b, h2_ready)

            def route_logits(b):
                dve.wait_ge(t0_filled, uses_up_to(T0_ORDER, ("router", b)))
                dve.wait_ge(ld_row, 16)
                nc.vector.scalar_tensor_tensor(rt[:, b, 0, :], T0[:, 0:E], 1.0 / S, br,
                                               ALU.mult, ALU.add).then_inc(t0_read, 1)
                dve.wait_ge(t0_read, reads_up_to(T0_ORDER, ("router", b)))
                link(nc.vector.reduce_max(sc[:, b, 0:1], rt[:, b, 0, :], axis=AX.X))
                nc.vector.tensor_scalar(rt[:, b, 1, :], rt[:, b, 0, :], sc[:, b, 0:1], None,
                                        ALU.subtract).then_inc(z_ready, 1)

            def route_top(b):
                dve.wait_ge(ez_ready, 2 * b + 1)
                link(nc.vector.reduce_sum(sc[:, b, 1:2], rt[:, b, 2, :], axis=AX.X))
                link(nc.vector.reciprocal(sc[:, b, 4:5], sc[:, b, 1:2]))
                link(nc.vector.tensor_scalar(rt[:, b, 3, :], rt[:, b, 2, :], sc[:, b, 4:5], None, ALU.mult))
                link(nc.vector.max(top[:, b, :], rt[:, b, 3, :]))
                nc.vector.tensor_tensor(sc[:, b, 2:3], top[:, b, 1:2], top[:, b, 0:1],
                                        ALU.subtract).then_inc(z_ready, 1)
                link(nc.vector.max_index(idx[:, b, :], top[:, b, :], rt[:, b, 3, :]))

            def route_shares(b):
                dve.wait_ge(ez_ready, 2 * b + 2)
                link(nc.vector.tensor_scalar(sc[:, b, 7:8], sc[:, b, 3:4], 1.0, None, ALU.add))
                link(nc.vector.reciprocal(sc[:, b, 5:6], sc[:, b, 7:8]))
                nc.vector.tensor_tensor(sc[:, b, 6:7], sc[:, b, 5:6], sc[:, b, 3:4], ALU.mult).then_inc(chosen, 1)
                dve.wait_ge(chosen, b + 1)

            chosen_expert = {}

            def pick_up(b, s):
                dve.wait_ge(ld_w1, 16)
                dve.wait_ge(ld_col, 16)
                e = nc.vector.value_load(idx[0:1, b, s:s + 1], min_val=0, max_val=E - 1)
                nc.vector.tensor_copy(w1e[:, b, s, :], w1s[:, bass.ds(e * F, F)]).then_inc(w1e_ready, 1)
                nc.vector.tensor_copy(b1e[:, b, s, :], col[:, bass.ds(e * FT, FT)]).then_inc(w1e_ready, 1)
                chosen_expert[b, s] = e

            def pick_bias(b):
                b2 = [col[:, bass.ds(chosen_expert[b, s] + E * FT, 1)] for s in range(2)]
                link(nc.vector.tensor_scalar(b2e[:, b, 0:1], b2[0], sc[:, b, 5:6], None, ALU.mult))
                link(nc.vector.scalar_tensor_tensor(b2e[:, b, 1:2], b2[1], sc[:, b, 6:7], b2e[:, b, 0:1],
                                                    ALU.mult, ALU.add))

            def ffn_out(b):
                dve.wait_ge(down_done, b + 1)
                nc.vector.scalar_tensor_tensor(yT[:, b, :], downBank[b][:, 0:S], b2e[:, b, 1:2], h2T[:, b, :],
                                               ALU.add, ALU.add).then_inc(yT_ready, 1)

            def third_norm(b):
                dve.wait_ge(t1_filled, uses_up_to(T1_ORDER, ("yT", b)))
                norm_stats(2 * B + b, lambda t: T1[:, t * P:(t + 1) * P], b)

            def finish(b):
                n = 2 * B + b
                for t in range(QT):
                    k = b * QT + t
                    nc.vector.scalar_tensor_tensor(yg[:, k, :], T1[:, t * P:(t + 1) * P], mv[:, n, t, 0:1],
                                                   gam2[:, :], ALU.subtract, ALU.mult).then_inc(t1_read, 1)
                dve.wait_ge(rstd_ready, n + 1)
                dve.wait_ge(xo_ready, b + 1)
                for t in range(QT):
                    k = b * QT + t
                    dve.wait_ge(t1_read, reads_before(T1_ORDER, ("yT", b)) + t + 1)
                    nc.vector.scalar_tensor_tensor(yo[:, k, :], yg[:, k, :], rstd[:, n, t:t + 1], xo[:, k, :],
                                                   ALU.mult, ALU.add).then_inc(y_ready, 1)

            for k in range(CH):
                row_max(0, k)
            max_high(0)
            max_low(0)
            for i in range(UNITS):
                if i + 1 < UNITS:
                    row_max(i + 1, 0)
                qB_copy(i)
                what, n = SMALL_IN.get(i, (None, None))
                if i + 1 < UNITS:
                    row_max(i + 1, 1)
                    if SMALL_IN.get(i - 1) == ("proj", 0):
                        second_norm(0)
                    row_max(i + 1, 2)
                    row_max(i + 1, 3)
                if what == "O":
                    o_sums(n)
                if i + 1 < UNITS:
                    max_high(i + 1)
                if what == "O":
                    o_norm(n)
                if i + 1 < UNITS:
                    max_low(i + 1)
                if what == "proj":
                    residual(0)
            route_logits(0)
            o_sums(5)
            o_norm(5)
            route_top(0)
            o_sums(6)
            o_norm(6)
            route_shares(0)
            o_sums(7)
            o_norm(7)
            pick_up(0, 0)
            residual(1)
            second_norm(1)
            pick_up(0, 1)
            pick_bias(0)
            route_logits(1)
            route_top(1)
            pick_up(1, 0)
            route_shares(1)
            pick_up(1, 1)
            pick_bias(1)
            ffn_out(0)
            third_norm(0)
            finish(0)
            ffn_out(1)
            third_norm(1)
            finish(1)

        @block.tensor
        def _(pe):
            def kv_project(n):
                if n == 0:
                    pe.wait_ge(ld_w, 16)
                    pe.wait_ge(ld_c0, 16)
                if n == 2:
                    pe.wait_ge(ld_c1, 16)
                bank = bankA[n] if n < 2 else bankB[n - 2]
                for t in range(2):
                    last = nc.tensor.matmul(bank[:, t * 2 * D:(t + 1) * 2 * D],
                                            cT[:, (2 * n + t) * P:(2 * n + t + 1) * P], w[:, 0:2 * D],
                                            start=True, stop=True)
                last.then_inc(kvp_done, 1)

            def transposes(bank, sources, identity, done):
                for t, source in enumerate(sources):
                    last = nc.tensor.transpose(bank[:, t * P:(t + 1) * P], source, identity[:, :])
                last.then_inc(done, 1)

            def h_transpose(b):
                pe.wait_ge(ident_ready, 1)
                pe.wait_ge(h_ready, QT * (b + 1))
                bank, filled = (T1, t1_filled) if b == 0 else (T0, t0_filled)
                transposes(bank, [h[:, b * QT + t, :] for t in range(QT)], ident, filled)

            def q_project(b):
                bank, read = (bankA[2], t1_read) if b == 0 else (bankV, t0_read)
                pe.wait_ge(read, 1)
                for t in range(QT):
                    last = nc.tensor.matmul(bank[:, t * D:(t + 1) * D],
                                            hT[:, b * S + t * P:b * S + (t + 1) * P], w[:, 2 * D:3 * D],
                                            start=True, stop=True)
                last.then_inc(qp_done, 1)

            def stack(i):
                b, g = divmod(i, UPB)
                if i == 0:
                    pe.wait_ge(pads_ready, 2)
                    pe.wait_ge(qpads_ready, 1)
                if g == 0:
                    pe.wait_ge(kpart[b], 4)
                    pe.wait_ge(qpart[b], 4)
                pe.wait_ge(t0_read, reads_before(T0_ORDER, ("stack", i)))
                transposes(T0b, [kst[:, b * KT + t, g, :] for t in range(KT)]
                           + [qst[:, b * QT + t, g, :] for t in range(QT)], identb, t0_filled)

            def scores_a(i, k):
                c = CH * i + k
                j, t = divmod(k, QT)
                if k == 0:
                    pe.wait_ge(t0_read, reads_up_to(T0_ORDER, ("stack", i)))
                if c == 0:
                    pe.wait_ge(kf_ready, 2)
                    pe.wait_ge(vx_ready, 4)
                    pe.wait_ge(qf_ready, 1)
                if c >= 3:
                    pe.wait_ge(a_read, c - 2)
                nc.tensor.matmul(bankA[c % 3][:, :], qA[:, i % RING, j, t * P:(t + 1) * P], kT[:, i, :],
                                 start=True, stop=True).then_inc(a_filled, 1)

            def max_stack(i):
                b, g = divmod(i, UPB)
                pe.wait_ge(m_ready, i + 1)
                pe.wait_ge(t1_read, reads_before(T1_ORDER, ("max", i)))
                transposes(T1b, [qst[:, b * QT + t, g, :] for t in range(QT)], identb, t1_filled)

            def scores_b(i, k):
                c = CH * i + k
                j, half_ = divmod(k, 2)
                if k == 0:
                    pe.wait_ge(t1_read, reads_up_to(T1_ORDER, ("max", i)))
                if c == 0:
                    pe.wait_ge(kf_ready, 4)
                    pe.wait_ge(vx_ready, 8)
                if c >= 2:
                    pe.wait_ge(p_ready, c - 1)
                for t in range(2):
                    kt = 2 * half_ + t
                    last = nc.tensor.matmul(bankB[c % 2][:, t * S:(t + 1) * S],
                                            kT[j * HB:(j + 1) * HB, i, kt * P:(kt + 1) * P],
                                            qB[j * HB:(j + 1) * HB, i % RING, :], start=True, stop=True)
                last.then_inc(b_filled, 1)

            def values(q, kt):
                b, quad = divmod(q, QUADS // B)
                pe.wait_ge(p_ready, CH * (2 * q + 1) + 2 + kt // 2 + 1)
                if kt == 0:
                    if q == 0:
                        pe.wait_ge(qf_ready, 2)
                    else:
                        pe.wait_ge(oT_ready, q)
                for n in range(4):
                    last = nc.tensor.matmul(bankV[32 * n:32 * n + 32, 0:S], vx[:, b * KT + kt, 4 * quad + n, :],
                                            pr[:, q % 2, n, kt, :], start=(kt == 0), stop=(kt == KT - 1))
                if kt == KT - 1:
                    last.then_inc(pv_done, 1)

            def small(name):
                what, n = name
                pe.wait_ge(t0_read, reads_before(T0_ORDER, name))
                tokens = range(n * QT, (n + 1) * QT)
                if what == "O":
                    pe.wait_ge(oT_ready, n + 1)
                    transposes(T0, [oT[:, n % 2, t * P:(t + 1) * P] for t in range(QT)], ident, t0_filled)
                elif what == "attnT":
                    transposes(T0, [attn[:, t, :] for t in tokens], ident, t0_filled)
                elif what == "proj":
                    for t in range(QT):
                        last = nc.tensor.matmul(T0[:, t * D:(t + 1) * D], attnT[:, n, t * P:(t + 1) * P],
                                                w[:, 3 * D:4 * D], start=True, stop=True)
                    last.then_inc(t0_filled, 1)
                elif what == "h2T":
                    pe.wait_ge(h2_ready, QT * (n + 1))
                    transposes(T0, [h2[:, t, :] for t in tokens], ident, t0_filled)
                else:
                    pe.wait_ge(ld_col, 16)
                    nc.tensor.matmul(T0[:, 0:E], hsum[:, n:n + 1].broadcast_to([P, P]),
                                     col[:, E * FT + E:COLS], start=True, stop=True).then_inc(t0_filled, 1)

            def up(b, n):
                if n % FT == 0:
                    pe.wait_ge(w1e_ready, 4 * b + 2 * (n // FT + 1))
                before = 2 * FT * b + n - 4
                if before < 0:
                    pe.wait_ge(a_read, CH * UNITS)
                    pe.wait_ge(p_ready, CH * UNITS)
                else:
                    pe.wait_ge(hid_ready, before + 1)
                nc.tensor.matmul(upBank[n % 4][:, 0:S], w1e[:, b, n // FT, (n % FT) * P:(n % FT + 1) * P],
                                 h2T[:, b, :], start=True, stop=True).then_inc(up_done, 1)

            def down(b, n):
                if n % FT == 0:
                    pe.wait_ge(w2e_ready, 2 * b + n // FT + 1)
                if b == 1 and n == 0:
                    pe.wait_ge(oT_ready, QUADS)
                pe.wait_ge(hid_ready, 2 * FT * b + n + 1)
                last = nc.tensor.matmul(downBank[b][:, 0:S], w2e[:, b, n // FT, (n % FT) * P:(n % FT + 1) * P],
                                        hid[:, b, n, :], start=(n == 0), stop=(n == 2 * FT - 1))
                if n == 2 * FT - 1:
                    last.then_inc(down_done, 1)

            def y_transpose(b):
                pe.wait_ge(yT_ready, b + 1)
                pe.wait_ge(t1_read, reads_before(T1_ORDER, ("yT", b)))
                transposes(T1, [yT[:, b, t * P:(t + 1) * P] for t in range(QT)], ident, t1_filled)

            kv_project(0)
            kv_project(1)
            h_transpose(0)
            q_project(0)
            h_transpose(1)
            kv_project(2)
            kv_project(3)
            q_project(1)
            for i in range(RING):
                stack(i)
            for k in range(CH):
                scores_a(0, k)
            scores_a(1, 0)
            scores_a(1, 1)
            for i in range(UNITS):
                q, r = (i - 2) // 2, 2 * (i % 2)
                max_stack(i)
                if i + 1 < UNITS:
                    scores_a(i + 1, 2)
                if q >= 0:
                    values(q, r)
                if i + 1 < UNITS:
                    scores_a(i + 1, 3)
                scores_b(i, 0)
                if i in SMALL_IN:
                    small(SMALL_IN[i])
                scores_b(i, 1)
                if q >= 0:
                    values(q, r + 1)
                if i + 2 < UNITS:
                    scores_a(i + 2, 0)
                scores_b(i, 2)
                if i + 2 < UNITS:
                    scores_a(i + 2, 1)
                scores_b(i, 3)
                if i + RING < UNITS:
                    stack(i + RING)
            small(("O", 5))
            values(QUADS - 1, 0)
            values(QUADS - 1, 1)
            small(("O", 6))
            values(QUADS - 1, 2)
            values(QUADS - 1, 3)
            small(("O", 7))
            small(("attnT", 1))
            small(("proj", 1))
            for n in range(FT):
                up(0, n)
            small(("h2T", 1))
            small(("router", 1))
            for n in range(2 * FT):
                down(0, n)
                if n + FT < 2 * FT:
                    up(0, n + FT)
            up(1, 0)
            up(1, 1)
            y_transpose(0)
            up(1, 2)
            up(1, 3)
            for n in range(2 * FT):
                down(1, n)
                if n + FT < 2 * FT:
                    up(1, n + FT)
            y_transpose(1)


_OUT = "out_dram"


def kernel(**inputs):
    import numpy as np
    import concourse.bacc as bacc
    from concourse.bass_utils import run_bass_kernel_spmd

    a = {k: np.asarray(v) for k, v in inputs.items()}
    xa, ff = "L0_xattn_", "L0_ffn_"
    arrays = {
        "x_in": a["x"].reshape(B * QT, P, D).transpose(1, 0, 2).reshape(P, B * QT * D),
        "ctx_in": a["ctx_1024"].reshape(B * C, D).T,
        "w_in": np.concatenate([a[xa + n].T for n in ("Wk", "Wv", "Wq", "Wo")], axis=1),
        "w1_in": a[ff + "W1"].transpose(1, 0, 2).reshape(P, E * F),
        "w2_in": a[ff + "W2"].reshape(E, FT, P, D).transpose(2, 0, 1, 3).reshape(P, E * F),
        "cols_in": np.concatenate([a[ff + "b1"].reshape(E * FT, P).T, a[ff + "b2"].T, a[ff + "Wr"]], axis=1),
        "rows_in": np.concatenate([a[xa + "bq"], a[xa + "bk"], a[xa + "bv"], a[xa + "bo"], a[ff + "gamma"],
                                   a[ff + "beta"], a[ff + "br"], a["g_xattn"], a["g_ffn"]]),
    }
    arrays = {k: np.ascontiguousarray(v) for k, v in arrays.items()}
    nc = bacc.Bacc("TRN2", target_bir_lowering=False, num_devices=1)
    args = [nc.dram_tensor(k, v.shape, mybir.dt.from_np(v.dtype), kind="ExternalInput").ap()
            for k, v in arrays.items()]
    out = nc.dram_tensor(_OUT, (B * S, D), mybir.dt.float32, kind="ExternalOutput").ap()
    build(nc, *args, out)
    r = run_bass_kernel_spmd(nc, [arrays], core_ids=[0])
    return r.results[0][_OUT].reshape(B, S, D)
```

```python
import concourse.bass as bass
from concourse import mybir
from contextlib import ExitStack
import math

B, S, C, D = 2, 256, 512, 128
H, DK = 16, 8
E, F = 8, 512
P = 128
QT, KT = S // P, C // P
FT = F // P
UNITS = B * H // 2
UPB = UNITS // B
QUADS = UNITS // 2
HB = 64
MAXROW = 48
CH = 4
RING = 4
GROUP = 2
GROUPS = UNITS // GROUP
AHEAD = 4
W1_AFTER = 6
SMALLEST_LOG = math.log(2.0 ** -126)
WARM = 8
SCALE = 1.0 / math.sqrt(DK)
EPS = 1e-5
ROWS = 6 * D + E + 2
COLS = E * FT + E + E

SMALL_IN = {4: ("O", 0), 6: ("O", 1), 8: ("O", 2), 10: ("O", 3), 11: ("attnT", 0), 12: ("proj", 0),
            13: ("O", 4), 14: ("h2T", 0), 15: ("O", 5)}
SMALL_AT_END = {14: ("router", 0)}
PROJ_STEP = next(_i for _i in SMALL_IN if SMALL_IN[_i] == ("proj", 0))
T0_ORDER = [("hT", 1)] + [("stack", _i) for _i in range(GROUP)]
for _i in range(UNITS):
    T0_ORDER += [SMALL_IN[_i]] if _i in SMALL_IN else []
    T0_ORDER += [SMALL_AT_END[_i]] if _i in SMALL_AT_END else []
T0_ORDER += [("O", 6), ("O", 7), ("attnT", 1), ("proj", 1), ("h2T", 1), ("router", 1)]
T1_ORDER = [("hT", 0)] + [("max", _i) for _i in range(UNITS)]
READERS = {"stack": 3}


def uses_up_to(order, name):
    return order.index(name) + 1


def reads_before(order, name):
    return sum(READERS.get(n, 1) for n, _ in order[:order.index(name)])


def reads_up_to(order, name):
    return reads_before(order, name) + READERS.get(name[0], 1)


def build(nc, x, ctxT, wqkvo, w1, w2, cols, rows, out):
    f32, bf16, u32 = mybir.dt.float32, mybir.dt.bfloat16, mybir.dt.uint32
    ALU, ACT, AX = mybir.AluOpType, mybir.ActivationFunctionType, mybir.AxisListType
    ctx = ExitStack()
    with ctx:
        def sb(name, shape, dt=f32):
            return ctx.enter_context(nc.sbuf_tensor(name, shape, dt))

        def ps(name, shape, dt=f32):
            return ctx.enter_context(nc.psum_tensor(name, shape, dt))

        def sem(name):
            return ctx.enter_context(nc.semaphore(name))

        xs = sb("xs", [P, B * QT, D])
        cT = sb("cT", [P, B * KT * P])
        w = sb("w", [P, 4 * D])
        w1s = sb("w1s", [P, E * F])
        w2s = sb("w2s", [P, E * F])
        col = sb("col", [P, COLS])
        row = sb("row", [P, ROWS])
        bk, bv, bq, bo, gamma, beta = (row[:, n * D:(n + 1) * D] for n in (1, 2, 0, 3, 4, 5))
        br = row[:, 6 * D:6 * D + E]
        gates = row[:, 6 * D + E:ROWS]
        ident = sb("ident", [P, P])
        identb = sb("identb", [P, P], bf16)
        ones = sb("ones", [1, P])
        tproj = sb("tproj", [P, S])
        tg = sb("tg", [P, 2])
        xg = sb("xg", [P, B * QT, D])
        gam2 = sb("gam2", [P, D])
        bet2 = sb("bet2", [P, D])
        half = sb("half", [P, QT])
        gelu_warm = sb("gelu_warm", [P, 1])
        euler = sb("euler", [P, E])
        LN = 3 * B
        stats = sb("stats", [P, LN, QT, 6])
        mv = sb("mv", [P, LN, QT, 2])
        veps = sb("veps", [P, LN, QT])
        rstd = sb("rstd", [P, LN, QT])
        h = sb("h", [P, B * QT, D])
        hT = sb("hT", [P, B * S])
        qf = sb("qf", [P, UNITS, QT, 2 * DK])
        qr = sb("qr", [P, UNITS, QT, 2 * DK])
        kf = sb("kf", [P, UNITS, KT, 2 * DK])
        kr = sb("kr", [P, UNITS, KT, 2 * DK])
        qst = sb("qst", [P, UNITS, QT, P], bf16)
        kst = sb("kst", [P, UNITS, KT, P], bf16)
        qT = sb("qT", [P, 2, GROUP, S], bf16)
        kT = sb("kT", [P, UNITS, C], bf16)
        qA = sb("qA", [P, RING, 2, S], bf16)
        qB = sb("qB", [P, RING, S], bf16)
        vx = sb("vx", [P, B * KT, H, DK + 1])
        nmax = sb("nmax", [P, UNITS, CH])
        pr = sb("pr", [P, 2, 4, KT, S])
        oT = sb("oT", [P, 2, S])
        rs = sb("rs", [P, QUADS, QT, 4])
        attn = sb("attn", [P, B * QT, D])
        attnT = sb("attnT", [P, B, S])
        tbo = sb("tbo", [P, D])
        x2 = sb("x2", [P, B * QT, D])
        xo = sb("xo", [P, B * QT, D])
        h2 = sb("h2", [P, B * QT, D])
        h2T = sb("h2T", [P, B, S])
        hsum = sb("hsum", [P, B])
        rt = sb("rt", [P, B, 8, E])
        top = sb("top", [P, B, E])
        largest = sb("largest", [P, B, 2, E])
        idx = sb("idx", [P, B, E], u32)
        sc = sb("sc", [P, B, 16])
        w1e = sb("w1e", [P, B, 2, F])
        w2e = sb("w2e", [P, B, 2, F])
        b1e = sb("b1e", [P, B, 2, FT])
        b2e = sb("b2e", [P, B, 2])
        hid = pr[:, 0, :, :, :].rearrange("p h k s -> p (h k) s").rearrange("p (b n) s -> p b n s", b=B)
        zT = sb("zT", [P, B, S])
        yg = sb("yg", [P, B * QT, D])
        yo = sb("yo", [P, B * QT, D])

        bankA = [ps(f"bankA{n}", [P, 512]) for n in range(3)]
        bankB = [ps(f"bankB{n}", [P, 512]) for n in range(2)]
        bankV = ps("bankV", [P, 512])
        T0 = ps("T0", [P, 512])
        T1 = ps("T1", [P, 512])
        T0b = T0[:, :].bitcast(bf16)
        T1b = T1[:, :].bitcast(bf16)

        ld_x, ld_w, ld_row, ld_c0, ld_c1 = sem("ld_x"), sem("ld_w"), sem("ld_row"), sem("ld_c0"), sem("ld_c1")
        ld_col, ld_w1, ld_w2 = sem("ld_col"), sem("ld_w1"), sem("ld_w2")
        stored = sem("stored")
        ident_ready = sem("ident_ready")
        ones_ready = sem("ones_ready")
        consts_ready = sem("consts_ready")
        pads_ready = sem("pads_ready")
        tanh_ready = sem("tanh_ready")
        folded = sem("folded")
        veps_ready, rstd_ready = sem("veps_ready"), sem("rstd_ready")
        h_ready = sem("h_ready")
        qp_done, kp_done, vp_done = sem("qp_done"), sem("kp_done"), sem("vp_done")
        qf_ready, kf_ready, vx_ready = sem("qf_ready"), sem("kf_ready"), sem("vx_ready")
        k_transposed, q_transposed = sem("k_transposed"), sem("q_transposed")
        w1e_last = sem("w1e_last")
        x2_ready = sem("x2_ready")
        q_masked = [sem("q_masked_even"), sem("q_masked_odd")]
        kpart = [sem(f"kpart{n}") for n in range(GROUPS)]
        qpart = [sem(f"qpart{n}") for n in range(GROUPS)]
        t0_filled, t0_read = sem("t0_filled"), sem("t0_read")
        t1_filled, t1_read = sem("t1_filled"), sem("t1_read")
        a_filled, a_read = sem("a_filled"), sem("a_read")
        m_high, m_ready = sem("m_high"), sem("m_ready")
        qmask_ready = sem("qmask_ready")
        qpads_ready = sem("qpads_ready")
        v_zero = sem("v_zero")
        b_filled, p_ready = sem("b_filled"), sem("p_ready")
        pv_done, oT_ready = sem("pv_done"), sem("oT_ready")
        rs_ready = sem("rs_ready")
        h2_ready = sem("h2_ready")
        xo_ready = sem("xo_ready")
        z_ready, ez_ready = sem("z_ready"), sem("ez_ready")
        idx_ready, chosen = sem("idx_ready"), sem("chosen")
        w1e_ready, w2e_ready = sem("w1e_ready"), sem("w2e_ready")
        up_done, hid_ready, down_done = sem("up_done"), sem("hid_ready"), sem("down_done")
        zT_ready = sem("zT_ready")
        gelu_loaded = sem("gelu_loaded")
        yg_ready, y_ready = sem("yg_ready"), sem("y_ready")
        chain = sem("chain")
        pchain = sem("pchain")

        upBank = [bankA[0], bankA[1], bankA[2], bankB[1]]
        downBank = [[bankB[0], T1], [bankV, T0]]

        kst_blocks = kst[:, :, :, :].rearrange("p u t (j c) -> p (u t j) c", c=HB)
        qst_blocks = qst[:, :, :, :].rearrange("p u t (j c) -> p (u t j) c", c=HB)

        kBank, vBank, qBank = [bankA[0], bankA[1]], [bankB[0], T1], [bankA[2], bankB[1]]

        def heads(t, group, tiles):
            return t[:, group * GROUP:(group + 1) * GROUP].rearrange("p u t (j d) -> p (u t j) d", d=DK)

        def slots(blocks, group, tiles, first, step, count):
            n = GROUP * tiles * 2
            part = blocks[:, group * n:(group + 1) * n, 0:MAXROW].rearrange("p n (s d) -> p n s d", d=DK)
            return part[:, :, first:first + step * (count - 1) + 1:step, :]

        def over(a, count):
            return a.unsqueeze(2).broadcast_to([P, a.shape[1], count, DK])

        QPARTS = [(0, 1, 3), (3, 2, 2), (4, 1, 1)]
        KPARTS = [(2, 1, 3), (1, 4, 2), (0, 1, 1)]

        def cut(step, copy, sub, group, keys):
            blocks, full, rest, tiles, parts = ((kst_blocks, kf, kr, KT, KPARTS) if keys else
                                                (qst_blocks, qf, qr, QT, QPARTS))
            high = slots(blocks, group, tiles, *parts[0])
            mid = slots(blocks, group, tiles, *parts[1])
            low = slots(blocks, group, tiles, *parts[2])
            v, r = heads(full, group, tiles), heads(rest, group, tiles)
            if step == 0:
                return copy(high, over(v, 3))
            if step == 1:
                return sub(r, v, high[:, :, 0, :])
            if step == 2:
                return copy(mid, over(r, 2))
            return sub(low[:, :, 0, :], r, mid[:, :, 0, :])

        block = ctx.enter_context(nc.Block())

        @block.sync
        def _(sp):
            sp.dma_start(xs[:, :, :], x.rearrange("p (t d) -> p t d", d=D)).then_inc(ld_x, 16)
            sp.dma_start(cT[:, 0:C], ctxT[:, 0:C]).then_inc(ld_c0, 16)
            sp.dma_start(cT[:, C:2 * C], ctxT[:, C:2 * C]).then_inc(ld_c1, 16)
            sp.dma_start(col[:, :], cols).then_inc(ld_col, 16)
            sp.wait_ge(pads_ready, 2)
            sp.wait_ge(qpads_ready, 1)
            sp.wait_ge(qmask_ready, 1)

            def mask_queries(group):
                sp.wait_ge(q_transposed, 16 * group)
                first = group * GROUP % RING
                if group * GROUP >= RING:
                    sp.wait_ge(a_filled, CH * (group * GROUP - RING + GROUP))
                for j in range(2):
                    half_ = slice(j * HB, (j + 1) * HB)
                    sp.dma_start(qA[half_, first:first + GROUP, j, :],
                                 qT[half_, group % 2, :, :]).then_inc(q_masked[group % 2], 16)

            for group in range(1, GROUPS):
                units = slice(group * GROUP, (group + 1) * GROUP)
                sp.wait_ge(qpart[group], 4)
                if group > 2:
                    sp.wait_ge(q_masked[group % 2], 32 * ((group - 1) // 2))
                sp.dma_start_transpose(qT[:, group % 2, :, :].rearrange("p u (t s) -> p (u t) s", s=P),
                                       qst[:, units, :, :].rearrange("p u t c -> p (u t c)")).then_inc(q_transposed, 16)
                sp.wait_ge(kpart[group], 4)
                if group > 1:
                    sp.wait_ge(k_transposed, 16 * (group - 1))
                sp.dma_start_transpose(kT[:, units, :].rearrange("p u (t s) -> p (u t) s", s=P),
                                       kst[:, units, :, :].rearrange("p u t c -> p (u t c)")).then_inc(k_transposed, 16)
                mask_queries(group)
                if group == W1_AFTER:
                    sp.dma_start(w1s[:, :], w1).then_inc(ld_w1, 16)
            sp.dma_start(w2s[:, :], w2).then_inc(ld_w2, 16)
            for b in range(B):
                for t in range(QT):
                    n = b * QT + t
                    sp.wait_ge(y_ready, n + 1)
                    sp.dma_start(out[n * P:(n + 1) * P, :], yo[:, n, :]).then_inc(stored, 16)
            sp.wait_ge(stored, 16 * B * QT)

        @block.gpsimd
        def _(pool):
            steps = [0]

            def link(ins):
                steps[0] += 1
                ins.then_inc(pchain, 1)
                pool.wait_ge(pchain, steps[0])

            pool.memset(half[:, :], -0.5).then_inc(consts_ready, 1)
            pool.memset(ones[:, :], 1.0).then_inc(ones_ready, 1)
            link(pool.memset(ident[:, :], 0.0))
            link(pool.affine_select(out=ident[:, :], in_=ident[:, :], compare_op=ALU.not_equal, fill=1.0,
                                    base=0, pattern=[[-1, P]], channel_multiplier=1))
            pool.tensor_copy(identb[:, :], ident[:, :]).then_inc(ident_ready, 1)
            pool.memset(kst_blocks[:, :, MAXROW:MAXROW + 2], 1.0).then_inc(pads_ready, 1)
            pool.memset(kst_blocks[:, :, MAXROW + 2:HB], 0.0).then_inc(pads_ready, 1)
            pool.memset(euler[:, :], math.e).then_inc(consts_ready, 1)

            def power(base, exponent, result, done):
                pool.tensor_tensor(result, base, exponent, ALU.pow).then_inc(done, 1)

            pool.wait_ge(consts_ready, 2)
            for b in range(B):
                pool.wait_ge(veps_ready, b + 1)
                power(veps[:, b, :], half[:, :], rstd[:, b, :], rstd_ready)
            pool.memset(vx[:, :, :, DK:DK + 1], 1.0).then_inc(pads_ready, 1)
            for group in range(2, GROUPS):
                b = group * GROUP // UPB
                for keys, ready, part in ((False, qf_ready, qpart[group]), (True, kf_ready, kpart[group])):
                    pool.wait_ge(ready, b + 1)
                    for s in range(4):
                        if s:
                            pool.wait_ge(part, s)
                        cut(s, pool.tensor_copy,
                            lambda o, a, c: pool.tensor_tensor(o, a, c, ALU.subtract),
                            group, keys).then_inc(part, 1)
            pool.wait_ge(ld_row, 16)
            pool.wait_ge(tanh_ready, 1)
            pool.wait_ge(ld_x, 16)
            pool.tensor_scalar(gam2[:, :], gamma, tg[:, 1:2], None, ALU.mult).then_inc(folded, 1)
            pool.tensor_scalar(bet2[:, :], beta, tg[:, 1:2], None, ALU.mult).then_inc(folded, 1)
            link(pool.tensor_scalar(tbo[:, :], bo, tg[:, 0:1], None, ALU.mult))
            pool.tensor_tensor(xg[:, :, :], xs[:, :, :], tbo[:, :].unsqueeze(1).broadcast_to([P, B * QT, D]),
                               ALU.add).then_inc(folded, 1)

            def router_powers(b):
                pool.wait_ge(z_ready, 2 * b + 1)
                power(euler[:, :], rt[:, b, 1, :], rt[:, b, 2, :], ez_ready)
                pool.wait_ge(z_ready, 2 * b + 2)
                power(euler[:, 0:1], sc[:, b, 2:3], sc[:, b, 3:4], ez_ready)

            def norm_power(n):
                pool.wait_ge(veps_ready, n + 1)
                power(veps[:, n, :], half[:, :], rstd[:, n, :], rstd_ready)

            def output_base(b):
                if b == 0:
                    pool.wait_ge(x2_ready, 1)
                else:
                    pool.wait_ge(t0_read, reads_up_to(T0_ORDER, ("proj", b)))
                pool.wait_ge(folded, 3)
                pool.tensor_tensor(xo[:, b * QT:(b + 1) * QT, :], x2[:, b * QT:(b + 1) * QT, :],
                                   bet2[:, :].unsqueeze(1).broadcast_to([P, QT, D]), ALU.add).then_inc(xo_ready, 1)

            pool.wait_ge(t0_read, reads_up_to(T0_ORDER, ("proj", 0)))
            pool.wait_ge(folded, 3)
            pool.tensor_tensor(x2[:, 0:QT, :], tproj[:, :].rearrange("p (t d) -> p t d", d=D), xg[:, 0:QT, :],
                               ALU.add).then_inc(x2_ready, 1)
            norm_power(B)
            output_base(0)
            router_powers(0)
            norm_power(B + 1)
            output_base(1)
            router_powers(1)
            for b in range(B):
                for t in range(QT):
                    pool.wait_ge(veps_ready, 2 * B + b * QT + t + 1)
                    power(veps[:, 2 * B + b, t:t + 1], half[:, 0:1], rstd[:, 2 * B + b, t:t + 1], rstd_ready)

        @block.scalar
        def _(act):
            def act_copy(o, a):
                return nc.scalar.activation(o, a, ACT.Copy)

            act.dma_start(w[:, :], wqkvo).then_inc(ld_w, 16)
            act.dma_start(row[:, :], rows.partition_broadcast(P)).then_inc(ld_row, 16)
            act.wait_ge(ld_row, 16)
            nc.scalar.activation(tg[:, :], gates, ACT.Tanh).then_inc(tanh_ready, 1)
            for b in range(B):
                bank, filled, read, use = (T1, t1_filled, t1_read, 1) if b == 0 else (T0, t0_filled, t0_read, 1)
                act.wait_ge(filled, use)
                act_copy(hT[:, b * S:(b + 1) * S], bank[:, 0:S]).then_inc(read, 1)
            act.wait_ge(qf_ready, 1)
            cut(0, act_copy, None, 0, False).then_inc(qpart[0], 1)
            act.wait_ge(kpart[0], 2)
            cut(2, act_copy, None, 0, True).then_inc(kpart[0], 1)
            act.wait_ge(qpart[0], 2)
            cut(2, act_copy, None, 0, False).then_inc(qpart[0], 1)

            def v_copy(b):
                act.wait_ge(vp_done, b + 1)
                if b == 0:
                    act.wait_ge(pads_ready, 3)
                act_copy(vx[:, b * KT:(b + 1) * KT, :, 0:DK],
                         vBank[b][:, :].rearrange("p (t h d) -> p t h d", t=KT, d=DK)).then_inc(vx_ready, 1)

            def stack_copy(i):
                act.wait_ge(t0_filled, uses_up_to(T0_ORDER, ("stack", i)))
                act_copy(kT[:, i, :], T0b[:, 0:C]).then_inc(t0_read, 1)
                if i == 0:
                    act.wait_ge(qmask_ready, 1)
                for j in range(2):
                    act_copy(qA[j * HB:(j + 1) * HB, i % RING, j, :],
                             T0b[j * HB:(j + 1) * HB, C:C + S]).then_inc(t0_read, 1)

            def qB_copy(i):
                act.wait_ge(t1_filled, uses_up_to(T1_ORDER, ("max", i)))
                if i >= RING:
                    act.wait_ge(b_filled, CH * (i - RING + 1))
                act_copy(qB[:, i % RING, :], T1b[:, 0:S]).then_inc(t1_read, 1)

            def exps(i, k):
                q, j, half_ = i // 2, k // 2, k % 2
                act.wait_ge(b_filled, CH * i + k + 1)
                if q >= 2:
                    act.wait_ge(pv_done, q - 1)
                nc.scalar.activation(
                    pr[:, q % 2, (i % 2) * 2 + j, 2 * half_:2 * half_ + 2, :],
                    bankB[k % 2][:, :].rearrange("p (t s) -> p t s", t=2),
                    ACT.Exp, scale=SCALE).then_inc(p_ready, 1)

            def o_copy(q):
                act.wait_ge(pv_done, q + 1)
                if q >= 2:
                    act.wait_ge(t0_filled, uses_up_to(T0_ORDER, ("O", q - 2)))
                act_copy(oT[:, q % 2, :], bankV[:, 0:S]).then_inc(oT_ready, 1)

            def attnT_copy(b):
                act.wait_ge(t0_filled, uses_up_to(T0_ORDER, ("attnT", b)))
                act_copy(attnT[:, b, :], T0[:, 0:S]).then_inc(t0_read, 1)

            def h2T_copy(b):
                act.wait_ge(t0_filled, uses_up_to(T0_ORDER, ("h2T", b)))
                nc.scalar.activation(h2T[:, b, :], T0[:, 0:S], ACT.Copy,
                                     accum_out=hsum[:, b:b + 1]).then_inc(t0_read, 1)

            def load_experts(b):
                act.wait_ge(idx_ready, b + 1)
                return [nc.scalar.value_load(idx[0:1, b, s:s + 1], min_val=0, max_val=E - 1) for s in range(2)]

            def pick_up_last(experts):
                act.wait_ge(ld_w1, 16)
                act.wait_ge(ld_col, 16)
                e = experts[1]
                act_copy(w1e[:, 1, 1, 0:P], w1s[:, bass.ds(e * F, P)]).then_inc(w1e_last, 1)
                act_copy(b1e[:, 1, 1, :], col[:, bass.ds(e * FT, FT)]).then_inc(w1e_last, 1)
                act_copy(w1e[:, 1, 1, P:F], w1s[:, bass.ds(e * F + P, F - P)]).then_inc(w1e_last, 1)

            def pick_down(b, s, experts):
                act.wait_ge(chosen, b + 1)
                act.wait_ge(ld_w2, 16)
                e = experts[s]
                nc.scalar.activation(w2e[:, b, s, :], w2s[:, bass.ds(e * F, F)], ACT.Copy,
                                     scale=sc[:, b, 5 + s:6 + s]).then_inc(w2e_ready, 1)

            def gelu(b, n):
                act.wait_ge(up_done, 2 * FT * b + n + 1)
                if b == 1 and n == FT:
                    act.wait_ge(w1e_last, 2)
                elif n % FT == 0:
                    act.wait_ge(w1e_ready, 6 * b + 3 * (n // FT + 1))
                nc.scalar.activation(hid[:, b, n, :], upBank[n % 4][:, 0:S], ACT.Gelu,
                                     bias=b1e[:, b, n // FT, n % FT:n % FT + 1]).then_inc(hid_ready, 1)

            stack_copy(0)
            v_copy(0)
            stack_copy(1)
            v_copy(1)
            qB_copy(0)
            for i in range(UNITS):
                exps(i, 0)
                exps(i, 1)
                if i >= 3 and i % 2 == 1:
                    o_copy((i - 3) // 2)
                if SMALL_IN.get(i) == ("attnT", 0):
                    attnT_copy(0)
                if SMALL_IN.get(i) == ("proj", 0):
                    act.wait_ge(t0_filled, uses_up_to(T0_ORDER, ("proj", 0)))
                    nc.scalar.activation(tproj[:, :], T0[:, 0:S], ACT.Copy, scale=tg[:, 0:1]).then_inc(t0_read, 1)
                if SMALL_IN.get(i) == ("h2T", 0):
                    h2T_copy(0)
                exps(i, 2)
                if i + 1 < UNITS:
                    qB_copy(i + 1)
                exps(i, 3)
            nc.scalar.activation(gelu_warm[:, :], half[:, 0:1], ACT.Gelu).then_inc(gelu_loaded, 1)
            experts = load_experts(0)
            o_copy(7)
            gelu(0, 0)
            gelu(0, 1)
            attnT_copy(1)
            pick_down(0, 0, experts)
            gelu(0, 2)
            gelu(0, 3)
            gelu(0, 4)
            pick_down(0, 1, experts)
            gelu(0, 5)
            gelu(0, 6)
            h2T_copy(1)
            gelu(0, 7)
            experts = load_experts(1)
            pick_up_last(experts)
            for n in range(2 * FT):
                if n == 4:
                    pick_down(1, 0, experts)
                if n == 6:
                    pick_down(1, 1, experts)
                gelu(1, n)

        @block.vector
        def _(dve):
            steps = [0]

            def link(ins):
                steps[0] += 1
                ins.then_inc(chain, 1)
                dve.wait_ge(chain, steps[0])

            def tile_stats(n, source):
                for t in range(QT):
                    steps[0] += 1
                    nc.vector.bn_stats(stats[:, n, t, :], source(t)).then_inc(chain, 1)

            def mean_and_variance(n):
                dve.wait_ge(chain, steps[0])
                for t in range(QT):
                    steps[0] += 1
                    nc.vector.bn_aggr(mv[:, n, t, :], stats[:, n, t, :]).then_inc(chain, 1)

            def variance_eps(n):
                dve.wait_ge(chain, steps[0])
                nc.vector.tensor_scalar(veps[:, n, :], mv[:, n, :, 1], EPS, None, ALU.add).then_inc(veps_ready, 1)

            def normalise(n, target, source, b, done):
                dve.wait_ge(rstd_ready, n + 1)
                for t in range(QT):
                    nc.vector.tensor_scalar(target[:, b * QT + t, :], source(t), mv[:, n, t, 0:1],
                                            rstd[:, n, t:t + 1], ALU.subtract, ALU.mult).then_inc(done, 1)

            nc.vector.memset(qA[:, :, :, :].rearrange("p r j s -> p (r j s)").bitcast(u32), 0).then_inc(qmask_ready, 1)
            nc.vector.memset(qst_blocks[:, :, MAXROW:HB], 0.0).then_inc(qpads_ready, 1)
            nc.vector.memset(bankV[:, 0:S], 0.0).then_inc(v_zero, 1)
            dve.wait_ge(ld_x, 16)
            for b in range(B):
                tile_stats(b, lambda t: xs[:, b * QT + t, :])
                mean_and_variance(b)
                variance_eps(b)
            for b in range(B):
                normalise(b, h, lambda t: xs[:, b * QT + t, :], b, h_ready)

            def by_unit(t):
                return t.rearrange("p t (g c) -> p t g c", c=2 * DK)

            def q_bias(b):
                dve.wait_ge(qp_done, b + 1)
                nc.vector.tensor_tensor(qf[:, b * UPB:(b + 1) * UPB].rearrange("p g t c -> p t g c"),
                                        by_unit(qBank[b][:, 0:S].rearrange("p (t d) -> p t d", d=D)),
                                        by_unit(bq.unsqueeze(1).broadcast_to([P, QT, D])),
                                        ALU.add).then_inc(qf_ready, 1)

            def k_bias(b):
                dve.wait_ge(kp_done, b + 1)
                nc.vector.tensor_tensor(kf[:, b * UPB:(b + 1) * UPB].rearrange("p g t c -> p t g c"),
                                        by_unit(kBank[b][:, :].rearrange("p (t d) -> p t d", d=D)),
                                        by_unit(bk.unsqueeze(1).broadcast_to([P, KT, D])),
                                        ALU.add).then_inc(kf_ready, 1)

            def sub(o, a, c):
                return nc.vector.tensor_tensor(o, a, c, ALU.subtract)

            dve.wait_ge(ld_row, 16)
            k_bias(0)
            dve.wait_ge(kf_ready, 1)
            cut(0, nc.vector.tensor_copy, sub, 0, True).then_inc(kpart[0], 1)
            q_bias(0)
            dve.wait_ge(kpart[0], 1)
            cut(1, None, sub, 0, True).then_inc(kpart[0], 1)
            dve.wait_ge(qpart[0], 1)
            cut(1, None, sub, 0, False).then_inc(qpart[0], 1)
            q_bias(1)
            dve.wait_ge(kpart[0], 3)
            cut(3, None, sub, 0, True).then_inc(kpart[0], 1)
            dve.wait_ge(qpart[0], 3)
            cut(3, None, sub, 0, False).then_inc(qpart[0], 1)
            for s in range(4):
                for keys, part in ((False, qpart[1]), (True, kpart[1])):
                    if s:
                        dve.wait_ge(part, s)
                    cut(s, nc.vector.tensor_copy, sub, 1, keys).then_inc(part, 1)
            k_bias(1)

            def row_max(i, k):
                c = CH * i + k
                dve.wait_ge(a_filled, c + 1)
                nc.vector.reduce_max(nmax[:, i, k:k + 1], bankA[c % 3][:, :], axis=AX.X,
                                     negate=True).then_inc(a_read, 1)

            def max_columns(i):
                return (qst[:, i].rearrange("p t (j c) -> p j t c", c=HB),
                        nmax[:, i, :].rearrange("p (j t) -> p j t", j=2))

            def max_high(i):
                columns, m = max_columns(i)
                dve.wait_ge(a_read, CH * (i + 1))
                nc.vector.tensor_copy(columns[:, :, :, MAXROW], m).then_inc(m_high, 1)

            def max_low(i):
                columns, m = max_columns(i)
                dve.wait_ge(m_high, i + 1)
                nc.vector.tensor_tensor(columns[:, :, :, MAXROW + 1], m, columns[:, :, :, MAXROW],
                                        ALU.subtract).then_inc(m_ready, 1)

            def o_sums(q):
                dve.wait_ge(t0_filled, uses_up_to(T0_ORDER, ("O", q)))
                o = T0[:, 0:S].rearrange("p (t h c) -> p t h c", t=QT, h=4)
                nc.vector.reciprocal(rs[:, q, :, :], o[:, :, :, DK]).then_inc(rs_ready, 1)

            def o_norm(q):
                b, quad = divmod(q, QUADS // B)
                o = T0[:, 0:S].rearrange("p (t h c) -> p t h c", t=QT, h=4)
                dve.wait_ge(rs_ready, q + 1)
                target = attn[:, b * QT:(b + 1) * QT, 32 * quad:32 * quad + 32]
                nc.vector.tensor_tensor(target.rearrange("p t (h d) -> p t h d", d=DK), o[:, :, :, 0:DK],
                                        rs[:, q, :, :].unsqueeze(3).broadcast_to([P, QT, 4, DK]),
                                        ALU.mult).then_inc(t0_read, 1)

            def residual(b):
                dve.wait_ge(t0_filled, uses_up_to(T0_ORDER, ("proj", b)))
                dve.wait_ge(folded, 3)
                t = slice(b * QT, (b + 1) * QT)
                nc.vector.scalar_tensor_tensor(x2[:, t, :], T0[:, 0:S].rearrange("p (t d) -> p t d", d=D),
                                               tg[:, 0:1], xg[:, t, :], ALU.mult, ALU.add).then_inc(t0_read, 1)

            def second_stats(b):
                if b == 0:
                    dve.wait_ge(x2_ready, 1)
                else:
                    dve.wait_ge(t0_read, reads_up_to(T0_ORDER, ("proj", b)))
                tile_stats(B + b, lambda t: x2[:, b * QT + t, :])

            def second_norm(b):
                normalise(B + b, h2, lambda t: x2[:, b * QT + t, :], b, h2_ready)

            def route_logits(b):
                dve.wait_ge(t0_filled, uses_up_to(T0_ORDER, ("router", b)))
                dve.wait_ge(ld_row, 16)
                nc.vector.scalar_tensor_tensor(rt[:, b, 0, :], T0[:, 0:E], 1.0 / S, br,
                                               ALU.mult, ALU.add).then_inc(t0_read, 1)
                dve.wait_ge(t0_read, reads_up_to(T0_ORDER, ("router", b)))
                link(nc.vector.max(largest[:, b, 0, :], rt[:, b, 0, :]))
                nc.vector.tensor_scalar(rt[:, b, 1, :], rt[:, b, 0, :], largest[:, b, 0, 0:1], SMALLEST_LOG,
                                        ALU.subtract, ALU.max).then_inc(z_ready, 1)
                link(nc.vector.tensor_scalar(largest[:, b, 1, :], largest[:, b, 0, :], largest[:, b, 0, 0:1],
                                             SMALLEST_LOG, ALU.subtract, ALU.max))
                dve.wait_ge(z_ready, 2 * b + 1)
                nc.vector.max_index(idx[:, b, :], largest[:, b, 1, :], rt[:, b, 1, :]).then_inc(idx_ready, 1)

            def route_top(b):
                dve.wait_ge(ez_ready, 2 * b + 1)
                link(nc.vector.reduce_sum(sc[:, b, 1:2], rt[:, b, 2, :], axis=AX.X))
                link(nc.vector.reciprocal(sc[:, b, 4:5], sc[:, b, 1:2]))
                link(nc.vector.tensor_scalar(rt[:, b, 3, :], rt[:, b, 2, :], sc[:, b, 4:5], None, ALU.mult))
                link(nc.vector.max(top[:, b, :], rt[:, b, 3, :]))
                nc.vector.tensor_tensor(sc[:, b, 2:3], top[:, b, 1:2], top[:, b, 0:1],
                                        ALU.subtract).then_inc(z_ready, 1)

            def route_shares(b):
                dve.wait_ge(ez_ready, 2 * b + 2)
                link(nc.vector.tensor_scalar(sc[:, b, 7:8], sc[:, b, 3:4], 1.0, None, ALU.add))
                link(nc.vector.reciprocal(sc[:, b, 5:6], sc[:, b, 7:8]))
                nc.vector.tensor_tensor(sc[:, b, 6:7], sc[:, b, 5:6], sc[:, b, 3:4], ALU.mult).then_inc(chosen, 1)
                dve.wait_ge(chosen, b + 1)

            chosen_expert = {}

            def load_expert(b, s):
                if s == 0:
                    dve.wait_ge(idx_ready, b + 1)
                chosen_expert[b, s] = nc.vector.value_load(idx[0:1, b, s:s + 1], min_val=0, max_val=E - 1)

            def pick_up(b, s):
                dve.wait_ge(ld_w1, 16)
                dve.wait_ge(ld_col, 16)
                load_expert(b, s)
                e = chosen_expert[b, s]
                nc.vector.tensor_copy(w1e[:, b, s, 0:P], w1s[:, bass.ds(e * F, P)]).then_inc(w1e_ready, 1)
                nc.vector.tensor_copy(w1e[:, b, s, P:F], w1s[:, bass.ds(e * F + P, F - P)]).then_inc(w1e_ready, 1)
                nc.vector.tensor_copy(b1e[:, b, s, :], col[:, bass.ds(e * FT, FT)]).then_inc(w1e_ready, 1)

            def pick_bias(b):
                b2 = [col[:, bass.ds(chosen_expert[b, s] + E * FT, 1)] for s in range(2)]
                link(nc.vector.tensor_scalar(b2e[:, b, 0:1], b2[0], sc[:, b, 5:6], None, ALU.mult))
                link(nc.vector.scalar_tensor_tensor(b2e[:, b, 1:2], b2[1], sc[:, b, 6:7], b2e[:, b, 0:1],
                                                    ALU.mult, ALU.add))

            def ffn_base(b):
                nc.vector.tensor_scalar(zT[:, b, :], h2T[:, b, :], b2e[:, b, 1:2], None, ALU.add).then_inc(zT_ready, 1)

            def third_norm(b, t):
                n, k = 2 * B + b, b * QT + t
                y = downBank[b][t][:, 0:D]
                dve.wait_ge(down_done, k + 1)
                link(nc.vector.bn_stats(stats[:, n, t, :], y))
                link(nc.vector.bn_aggr(mv[:, n, t, :], stats[:, n, t, :]))
                nc.vector.tensor_scalar(veps[:, n, t:t + 1], mv[:, n, t, 1:2], EPS, None, ALU.add).then_inc(veps_ready, 1)
                nc.vector.scalar_tensor_tensor(yg[:, k, :], y, mv[:, n, t, 0:1], gam2[:, :],
                                               ALU.subtract, ALU.mult).then_inc(yg_ready, 1)

            def finish(b, t):
                n, k = 2 * B + b, b * QT + t
                dve.wait_ge(xo_ready, b + 1)
                dve.wait_ge(yg_ready, k + 1)
                dve.wait_ge(rstd_ready, 2 * B + k + 1)
                nc.vector.scalar_tensor_tensor(yo[:, k, :], yg[:, k, :], rstd[:, n, t:t + 1], xo[:, k, :],
                                               ALU.mult, ALU.add).then_inc(y_ready, 1)

            for k in range(CH):
                row_max(0, k)
            max_high(0)
            max_low(0)
            for i in range(UNITS):
                if i + 1 < UNITS:
                    row_max(i + 1, 0)
                what, n = SMALL_IN.get(i, (None, None))
                norm_step = i - PROJ_STEP
                if i + 1 < UNITS:
                    row_max(i + 1, 1)
                    if norm_step == 1:
                        second_stats(0)
                    if norm_step == 2:
                        second_norm(0)
                    row_max(i + 1, 2)
                    if norm_step == 1:
                        mean_and_variance(B)
                    row_max(i + 1, 3)
                    if norm_step == 1:
                        variance_eps(B)
                if i == UNITS - 1:
                    route_logits(0)
                    pick_up(0, 0)
                if what == "O":
                    o_sums(n)
                if i + 1 < UNITS:
                    max_high(i + 1)
                if what == "O":
                    o_norm(n)
                if i + 1 < UNITS:
                    max_low(i + 1)
            route_top(0)
            pick_up(0, 1)
            o_sums(6)
            o_norm(6)
            route_shares(0)
            o_sums(7)
            o_norm(7)
            residual(1)
            second_stats(1)
            mean_and_variance(B + 1)
            variance_eps(B + 1)
            pick_bias(0)
            ffn_base(0)
            second_norm(1)
            route_logits(1)
            pick_up(1, 0)
            route_top(1)
            load_expert(1, 1)
            route_shares(1)
            pick_bias(1)
            ffn_base(1)
            for b in range(B):
                third_norm(b, 0)
                third_norm(b, 1)
                finish(b, 0)
                finish(b, 1)

        @block.tensor
        def _(pe):
            pe.wait_ge(qmask_ready, 1)
            for n in range(WARM):
                nc.tensor.matmul(bankB[0][:, :], qA[:, 0, 0, 0:P], qA[:, 0:1, :, :].rearrange("p r j s -> p (r j s)"),
                                 start=True, stop=True)

            def value_bias(b):
                pe.wait_ge(ones_ready, 1)
                pe.wait_ge(ld_row, 16)
                nc.tensor.matmul(vBank[b][:, :], ones[:, :], bv[0:1, :].unsqueeze(1).broadcast_to([1, KT, D]),
                                 start=True, stop=False)

            def context_project(b, banks, first, done, biased=False, tiles=range(KT)):
                for t in tiles:
                    last = nc.tensor.matmul(banks[b][:, t * D:(t + 1) * D],
                                            cT[:, (b * KT + t) * P:(b * KT + t + 1) * P], w[:, first:first + D],
                                            start=not biased, stop=(not biased or t == KT - 1))
                if tiles[-1] == KT - 1:
                    last.then_inc(done, 1)

            def transposes(bank, sources, identity, done):
                for t, source in enumerate(sources):
                    last = nc.tensor.transpose(bank[:, t * P:(t + 1) * P], source, identity[:, :])
                last.then_inc(done, 1)

            def h_transpose(b):
                pe.wait_ge(ident_ready, 1)
                pe.wait_ge(h_ready, QT * (b + 1))
                bank, filled = (T1, t1_filled) if b == 0 else (T0, t0_filled)
                transposes(bank, [h[:, b * QT + t, :] for t in range(QT)], ident, filled)

            def q_project(b):
                bank = qBank[b]
                pe.wait_ge(t1_read if b == 0 else t0_read, 1)
                for t in range(QT):
                    last = nc.tensor.matmul(bank[:, t * D:(t + 1) * D],
                                            hT[:, b * S + t * P:b * S + (t + 1) * P], w[:, 2 * D:3 * D],
                                            start=True, stop=True)
                last.then_inc(qp_done, 1)

            def stack(i):
                if i == 0:
                    pe.wait_ge(pads_ready, 2)
                    pe.wait_ge(qpads_ready, 1)
                if i % GROUP == 0:
                    pe.wait_ge(kpart[i // GROUP], 4)
                    pe.wait_ge(qpart[i // GROUP], 4)
                pe.wait_ge(t0_read, reads_before(T0_ORDER, ("stack", i)))
                transposes(T0b, [kst[:, i, t, :] for t in range(KT)] + [qst[:, i, t, :] for t in range(QT)],
                           identb, t0_filled)

            def scores_a(i, k):
                c = CH * i + k
                j, t = divmod(k, QT)
                if k == 0 and i < GROUP:
                    pe.wait_ge(t0_read, reads_up_to(T0_ORDER, ("stack", i)))
                if k == 0 and i >= GROUP:
                    group = i // GROUP
                    pe.wait_ge(k_transposed, 16 * group)
                    pe.wait_ge(q_masked[group % 2], 32 * ((group + 1) // 2))
                if c == 0:
                    pe.wait_ge(kf_ready, 2)
                    pe.wait_ge(qf_ready, 1)
                if c >= 3:
                    pe.wait_ge(a_read, c - 2)
                nc.tensor.matmul(bankA[c % 3][:, :], qA[:, i % RING, j, t * P:(t + 1) * P], kT[:, i, :],
                                 start=True, stop=True).then_inc(a_filled, 1)

            def max_stack(i):
                pe.wait_ge(m_ready, i + 1)
                if i == 0:
                    pe.wait_ge(vx_ready, 2)
                pe.wait_ge(t1_read, reads_before(T1_ORDER, ("max", i)))
                transposes(T1b, [qst[:, i, t, :] for t in range(QT)], identb, t1_filled)

            def scores_b(i, k):
                c = CH * i + k
                j, half_ = divmod(k, 2)
                if k == 0:
                    pe.wait_ge(t1_read, reads_up_to(T1_ORDER, ("max", i)))
                if c == 0:
                    pe.wait_ge(vx_ready, 1)
                    pe.wait_ge(qf_ready, 2)
                if c >= 2:
                    pe.wait_ge(p_ready, c - 1)
                for t in range(2):
                    kt = 2 * half_ + t
                    last = nc.tensor.matmul(bankB[c % 2][:, t * S:(t + 1) * S],
                                            kT[j * HB:(j + 1) * HB, i, kt * P:(kt + 1) * P],
                                            qB[j * HB:(j + 1) * HB, i % RING, :], start=True, stop=True)
                last.then_inc(b_filled, 1)

            def values(q, kt):
                b, quad = divmod(q, QUADS // B)
                pe.wait_ge(p_ready, CH * (2 * q + 1) + 2 + kt // 2 + 1)
                if kt == 0:
                    if q == 0:
                        pe.wait_ge(v_zero, 1)
                    else:
                        pe.wait_ge(oT_ready, q)
                for n in range(4):
                    last = nc.tensor.matmul(bankV[32 * n:32 * n + DK + 1, 0:S], vx[:, b * KT + kt, 4 * quad + n, :],
                                            pr[:, q % 2, n, kt, :], start=(kt == 0), stop=(kt == KT - 1))
                if kt == KT - 1:
                    last.then_inc(pv_done, 1)

            def small(name):
                what, n = name
                pe.wait_ge(t0_read, reads_before(T0_ORDER, name))
                tokens = range(n * QT, (n + 1) * QT)
                if what == "O":
                    pe.wait_ge(oT_ready, n + 1)
                    transposes(T0, [oT[:, n % 2, t * P:(t + 1) * P] for t in range(QT)], ident, t0_filled)
                elif what == "attnT":
                    transposes(T0, [attn[:, t, :] for t in tokens], ident, t0_filled)
                elif what == "proj":
                    for t in range(QT):
                        last = nc.tensor.matmul(T0[:, t * D:(t + 1) * D], attnT[:, n, t * P:(t + 1) * P],
                                                w[:, 3 * D:4 * D], start=True, stop=True)
                    last.then_inc(t0_filled, 1)
                elif what == "h2T":
                    pe.wait_ge(h2_ready, QT * (n + 1))
                    transposes(T0, [h2[:, t, :] for t in tokens], ident, t0_filled)
                else:
                    pe.wait_ge(ld_col, 16)
                    nc.tensor.matmul(T0[:, 0:E], hsum[:, n:n + 1].broadcast_to([P, P]),
                                     col[:, E * FT + E:COLS], start=True, stop=True).then_inc(t0_filled, 1)

            def up(b, n):
                if b == 1 and n // FT == 1:
                    if n % FT < 2:
                        pe.wait_ge(w1e_last, 2 * (n % FT) + 1)
                elif n % FT < 2:
                    pe.wait_ge(w1e_ready, 6 * b + 3 * (n // FT) + n % FT + 1)
                before = 2 * FT * b + n - 4
                if before < 0:
                    pe.wait_ge(a_read, CH * UNITS)
                    if n == 3:
                        pe.wait_ge(p_ready, CH * UNITS)
                else:
                    pe.wait_ge(hid_ready, before + 1)
                nc.tensor.matmul(upBank[n % 4][:, 0:S], w1e[:, b, n // FT, (n % FT) * P:(n % FT + 1) * P],
                                 h2T[:, b, :], start=True, stop=True).then_inc(up_done, 1)

            def down(b, n, tiles=range(QT)):
                if n % FT == 0:
                    pe.wait_ge(w2e_ready, 2 * b + n // FT + 1)
                if b == 0 and n == 0:
                    pe.wait_ge(t1_read, reads_up_to(T1_ORDER, ("max", UNITS - 1)))
                if b == 1 and n == 0:
                    pe.wait_ge(oT_ready, QUADS)
                    pe.wait_ge(t0_read, reads_up_to(T0_ORDER, ("router", 1)))
                pe.wait_ge(hid_ready, 2 * FT * b + n + 1)
                for t in tiles:
                    last = nc.tensor.matmul(downBank[b][t][:, 0:D], hid[:, b, n, t * P:(t + 1) * P],
                                            w2e[:, b, n // FT, (n % FT) * P:(n % FT + 1) * P],
                                            start=(n == 0), stop=(n == 2 * FT - 1))
                    if n == 2 * FT - 1:
                        last.then_inc(down_done, 1)

            def add_base(b):
                pe.wait_ge(zT_ready, b + 1)
                for t in range(QT):
                    nc.tensor.matmul(downBank[b][t][:, 0:D], zT[:, b, t * P:(t + 1) * P], ident[:, :],
                                     start=False, stop=False)

            def last_downs(b):
                add_base(b)
                for t in range(QT):
                    for n in range(FT, 2 * FT):
                        down(b, n, [t])

            pe.wait_ge(ld_w, 16)
            pe.wait_ge(ld_c0, 16)
            context_project(0, kBank, 0, kp_done, tiles=range(0, 2))
            h_transpose(0)
            context_project(0, kBank, 0, kp_done, tiles=range(2, KT))
            h_transpose(1)
            q_project(0)
            q_project(1)
            pe.wait_ge(ld_c1, 16)
            context_project(1, kBank, 0, kp_done)
            value_bias(0)
            stack(0)
            context_project(0, vBank, D, vp_done, biased=True)
            value_bias(1)
            scores_a(0, 0)
            scores_a(0, 1)
            stack(1)
            scores_a(0, 2)
            context_project(1, vBank, D, vp_done, biased=True)
            scores_a(0, 3)
            scores_a(1, 0)
            scores_a(1, 1)
            for i in range(UNITS):
                q, r = (i - 2) // 2, 2 * (i % 2)
                max_stack(i)
                if i + 1 < UNITS:
                    scores_a(i + 1, 2)
                if q >= 0:
                    values(q, r)
                if i + 1 < UNITS:
                    scores_a(i + 1, 3)
                scores_b(i, 0)
                scores_b(i, 1)
                if q >= 0:
                    values(q, r + 1)
                if i in SMALL_IN:
                    small(SMALL_IN[i])
                if i + 2 < UNITS:
                    scores_a(i + 2, 0)
                scores_b(i, 2)
                if i + 2 < UNITS:
                    scores_a(i + 2, 1)
                scores_b(i, 3)
                if i in SMALL_AT_END:
                    small(SMALL_AT_END[i])
            up(0, 0)
            values(QUADS - 1, 0)
            values(QUADS - 1, 1)
            small(("O", 6))
            values(QUADS - 1, 2)
            values(QUADS - 1, 3)
            up(0, 1)
            small(("O", 7))
            up(0, 2)
            small(("attnT", 1))
            up(0, 3)
            small(("proj", 1))
            for n in range(3):
                down(0, n)
                up(0, n + 4)
            add_base(0)
            small(("h2T", 1))
            down(0, 3)
            small(("router", 1))
            up(0, 7)
            down(0, 4)
            for t in range(QT):
                for n in range(5, 2 * FT):
                    down(0, n, [t])
            for n in range(FT + AHEAD):
                up(1, n)
            for n in range(FT):
                down(1, n)
                if n + FT + AHEAD < 2 * FT:
                    up(1, n + FT + AHEAD)
            last_downs(1)


_OUT = "out_dram"


def kernel(**inputs):
    import numpy as np
    import concourse.bacc as bacc
    from concourse.bass_utils import run_bass_kernel_spmd

    a = {k: np.asarray(v) for k, v in inputs.items()}
    xa, ff = "L0_xattn_", "L0_ffn_"
    arrays = {
        "x_in": a["x"].reshape(B * QT, P, D).transpose(1, 0, 2).reshape(P, B * QT * D),
        "ctx_in": a["ctx_1024"].reshape(B * C, D).T,
        "w_in": np.concatenate([a[xa + n].T for n in ("Wk", "Wv", "Wq", "Wo")], axis=1),
        "w1_in": a[ff + "W1"].transpose(1, 0, 2).reshape(P, E * F),
        "w2_in": a[ff + "W2"].reshape(E, FT, P, D).transpose(2, 0, 1, 3).reshape(P, E * F),
        "cols_in": np.concatenate([a[ff + "b1"].reshape(E * FT, P).T, a[ff + "b2"].T, a[ff + "Wr"]], axis=1),
        "rows_in": np.concatenate([a[xa + "bq"], a[xa + "bk"], a[xa + "bv"], a[xa + "bo"], a[ff + "gamma"],
                                   a[ff + "beta"], a[ff + "br"], a["g_xattn"], a["g_ffn"]]),
    }
    arrays = {k: np.ascontiguousarray(v) for k, v in arrays.items()}
    nc = bacc.Bacc("TRN2", target_bir_lowering=False, num_devices=1)
    args = [nc.dram_tensor(k, v.shape, mybir.dt.from_np(v.dtype), kind="ExternalInput").ap()
            for k, v in arrays.items()]
    out = nc.dram_tensor(_OUT, (B * S, D), mybir.dt.float32, kind="ExternalOutput").ap()
    build(nc, *args, out)
    r = run_bass_kernel_spmd(nc, [arrays], core_ids=[0])
    return r.results[0][_OUT].reshape(B, S, D)
```
